# Optimizing a Trainium2 kernel written in Bass

```python
import numpy as np
import jax
import jax.numpy as jnp

def _softmax(x, axis=-1):
    return jax.nn.softmax(x, axis=axis)
def _gelu(x):
    return jax.nn.gelu(x, approximate=True)
def _silu(x):
    return jax.nn.silu(x)
def _sigmoid(x):
    return jax.nn.sigmoid(x)
def _layernorm(x, axis=-1, eps=1e-5):
    m = jnp.mean(x, axis=axis, keepdims=True)
    v = jnp.var(x, axis=axis, keepdims=True)
    return (x - m) / jnp.sqrt(v + eps)
def _scatter_add(tgt, idx, src, axis=0):
    return tgt.at[idx].add(src)
def _segment_sum(src, seg, n):
    return jax.ops.segment_sum(src, seg, n)

kernel_name = 'mk_rec_standalone_d1_rec_ed7d42'

def setup_inputs(seed: int = 0):
    np.random.seed(seed)
    _w = jnp.asarray
    def _rec_inputs():
        import jax
        import jax.numpy as jnp
        _rk = jax.random.key(seed)
        r_item_mm = -0.000514642 + 1.00011 * jax.random.normal(jax.random.fold_in(_rk, 1), (16384, 128), jnp.float32)
        r_item_id = jax.random.randint(jax.random.fold_in(_rk, 2), (16384,), 4, 91708, jnp.int32)
        r_likes = jax.random.randint(jax.random.fold_in(_rk, 3), (16384,), 0, 11, jnp.int32)
        r_views = jax.random.randint(jax.random.fold_in(_rk, 4), (16384,), 0, 11, jnp.int32)
        r_item_seq = jnp.stack([jax.random.randint(jax.random.fold_in(jax.random.fold_in(_rk, 5), 0), (16384,), 12, 91708, jnp.int32), jax.random.randint(jax.random.fold_in(jax.random.fold_in(_rk, 5), 1), (16384,), 1, 91713, jnp.int32), jax.random.randint(jax.random.fold_in(jax.random.fold_in(_rk, 5), 2), (16384,), 0, 91714, jnp.int32), jax.random.randint(jax.random.fold_in(jax.random.fold_in(_rk, 5), 3), (16384,), 4, 91718, jnp.int32), jax.random.randint(jax.random.fold_in(jax.random.fold_in(_rk, 5), 4), (16384,), 4, 91715, jnp.int32), jax.random.randint(jax.random.fold_in(jax.random.fold_in(_rk, 5), 5), (16384,), 8, 91715, jnp.int32), jax.random.randint(jax.random.fold_in(jax.random.fold_in(_rk, 5), 6), (16384,), 14, 91718, jnp.int32), jax.random.randint(jax.random.fold_in(jax.random.fold_in(_rk, 5), 7), (16384,), 0, 91704, jnp.int32), jax.random.randint(jax.random.fold_in(jax.random.fold_in(_rk, 5), 8), (16384,), 2, 91718, jnp.int32), jax.random.randint(jax.random.fold_in(jax.random.fold_in(_rk, 5), 9), (16384,), 9, 91716, jnp.int32), jax.random.randint(jax.random.fold_in(jax.random.fold_in(_rk, 5), 10), (16384,), 7, 91718, jnp.int32), jax.random.randint(jax.random.fold_in(jax.random.fold_in(_rk, 5), 11), (16384,), 0, 91715, jnp.int32), jax.random.randint(jax.random.fold_in(jax.random.fold_in(_rk, 5), 12), (16384,), 8, 91718, jnp.int32), jax.random.randint(jax.random.fold_in(jax.random.fold_in(_rk, 5), 13), (16384,), 3, 91708, jnp.int32), jax.random.randint(jax.random.fold_in(jax.random.fold_in(_rk, 5), 14), (16384,), 2, 91710, jnp.int32), jax.random.randint(jax.random.fold_in(jax.random.fold_in(_rk, 5), 15), (16384,), 5, 91712, jnp.int32), jax.random.randint(jax.random.fold_in(jax.random.fold_in(_rk, 5), 16), (16384,), 7, 91717, jnp.int32), jax.random.randint(jax.random.fold_in(jax.random.fold_in(_rk, 5), 17), (16384,), 2, 91717, jnp.int32), jax.random.randint(jax.random.fold_in(jax.random.fold_in(_rk, 5), 18), (16384,), 1, 91712, jnp.int32), jax.random.randint(jax.random.fold_in(jax.random.fold_in(_rk, 5), 19), (16384,), 2, 91718, jnp.int32), jax.random.randint(jax.random.fold_in(jax.random.fold_in(_rk, 5), 20), (16384,), 0, 91717, jnp.int32), jax.random.randint(jax.random.fold_in(jax.random.fold_in(_rk, 5), 21), (16384,), 4, 91717, jnp.int32), jax.random.randint(jax.random.fold_in(jax.random.fold_in(_rk, 5), 22), (16384,), 4, 91718, jnp.int32), jax.random.randint(jax.random.fold_in(jax.random.fold_in(_rk, 5), 23), (16384,), 17, 91718, jnp.int32), jax.random.randint(jax.random.fold_in(jax.random.fold_in(_rk, 5), 24), (16384,), 4, 91718, jnp.int32), jax.random.randint(jax.random.fold_in(jax.random.fold_in(_rk, 5), 25), (16384,), 1, 91718, jnp.int32), jax.random.randint(jax.random.fold_in(jax.random.fold_in(_rk, 5), 26), (16384,), 0, 91718, jnp.int32), jax.random.randint(jax.random.fold_in(jax.random.fold_in(_rk, 5), 27), (16384,), 3, 91718, jnp.int32), jax.random.randint(jax.random.fold_in(jax.random.fold_in(_rk, 5), 28), (16384,), 15, 91712, jnp.int32), jax.random.randint(jax.random.fold_in(jax.random.fold_in(_rk, 5), 29), (16384,), 1, 91703, jnp.int32), jax.random.randint(jax.random.fold_in(jax.random.fold_in(_rk, 5), 30), (16384,), 1, 91715, jnp.int32), jax.random.randint(jax.random.fold_in(jax.random.fold_in(_rk, 5), 31), (16384,), 0, 91711, jnp.int32), jax.random.randint(jax.random.fold_in(jax.random.fold_in(_rk, 5), 32), (16384,), 1, 91705, jnp.int32), jax.random.randint(jax.random.fold_in(jax.random.fold_in(_rk, 5), 33), (16384,), 5, 91716, jnp.int32), jax.random.randint(jax.random.fold_in(jax.random.fold_in(_rk, 5), 34), (16384,), 0, 91710, jnp.int32), jax.random.randint(jax.random.fold_in(jax.random.fold_in(_rk, 5), 35), (16384,), 3, 91714, jnp.int32), jax.random.randint(jax.random.fold_in(jax.random.fold_in(_rk, 5), 36), (16384,), 23, 91696, jnp.int32), jax.random.randint(jax.random.fold_in(jax.random.fold_in(_rk, 5), 37), (16384,), 6, 91718, jnp.int32), jax.random.randint(jax.random.fold_in(jax.random.fold_in(_rk, 5), 38), (16384,), 0, 91706, jnp.int32), jax.random.randint(jax.random.fold_in(jax.random.fold_in(_rk, 5), 39), (16384,), 9, 91707, jnp.int32), jax.random.randint(jax.random.fold_in(jax.random.fold_in(_rk, 5), 40), (16384,), 21, 91713, jnp.int32), jax.random.randint(jax.random.fold_in(jax.random.fold_in(_rk, 5), 41), (16384,), 7, 91714, jnp.int32), jax.random.randint(jax.random.fold_in(jax.random.fold_in(_rk, 5), 42), (16384,), 9, 91711, jnp.int32), jax.random.randint(jax.random.fold_in(jax.random.fold_in(_rk, 5), 43), (16384,), 15, 91702, jnp.int32), jax.random.randint(jax.random.fold_in(jax.random.fold_in(_rk, 5), 44), (16384,), 0, 91716, jnp.int32), jax.random.randint(jax.random.fold_in(jax.random.fold_in(_rk, 5), 45), (16384,), 8, 91713, jnp.int32), jax.random.randint(jax.random.fold_in(jax.random.fold_in(_rk, 5), 46), (16384,), 5, 91715, jnp.int32), jax.random.randint(jax.random.fold_in(jax.random.fold_in(_rk, 5), 47), (16384,), 17, 91711, jnp.int32), jax.random.randint(jax.random.fold_in(jax.random.fold_in(_rk, 5), 48), (16384,), 0, 91716, jnp.int32), jax.random.randint(jax.random.fold_in(jax.random.fold_in(_rk, 5), 49), (16384,), 18, 91711, jnp.int32)], axis=1)
        return r_item_mm, r_item_id, r_likes, r_views, r_item_seq
    r_item_mm, r_item_id, r_likes, r_views, r_item_seq = _rec_inputs()
    def _L0_rec_setup():
        import jax, jax.numpy as jnp
        import numpy as np
        B, L, D, V, C = (16384, 50, 128, 91718, 11)
        H, HD, F = (4, 32, 6)
        NP = F * (F - 1) // 2
        CIN = F * D + NP * D

        def _forward(item_id, item_mm, likes, views, item_seq, item_emb, cate_emb, mm_w, mm_b, ln_g, ln_b, gnn_W, gnn_a, se_w1, se_b1, se_w2, se_b2, bi_W, mlp_w1, mlp_b1, bn1_g, bn1_b, mlp_w2, mlp_b2, bn2_g, bn2_b, mlp_w3, mlp_b3):
            bsz = item_id.shape[0]
            eps = 1e-05
            user_feat = jnp.zeros((bsz, D), item_mm.dtype)
            like_feat = cate_emb[likes]
            view_feat = cate_emb[views]
            id_feat = item_emb[item_id]
            y = item_mm @ mm_w + mm_b
            mu = y.mean(-1, keepdims=True)
            var = y.var(-1, keepdims=True)
            y = (y - mu) * jax.lax.rsqrt(var + eps) * ln_g + ln_b
            img_feat = jax.nn.gelu(y, approximate=False)
            seq_emb = item_emb[item_seq]
            mask = item_seq == 0
            seq_emb = jnp.where(mask[..., None], 0.0, seq_emb)
            cnt = jnp.clip(jnp.sum((~mask).astype(seq_emb.dtype), axis=1, keepdims=True), 1.0)
            hist_feat = seq_emb.sum(1) / cnt
            x = jnp.stack([user_feat, like_feat, view_feat, id_feat, img_feat, hist_feat], axis=1)
            hp = jnp.einsum('bni,hio->bnho', x, gnn_W)
            a1 = gnn_a[:, :HD, 0]
            a2 = gnn_a[:, HD:, 0]
            ei = jnp.einsum('bnhd,hd->bhn', hp, a1)
            ej = jnp.einsum('bnhd,hd->bhn', hp, a2)
            e = ei[:, :, :, None] + ej[:, :, None, :]
            e = jnp.where(e > 0, e, 0.2 * e)
            att = jax.nn.softmax(e, axis=-1)
            h_new = jnp.einsum('bhnm,bmho->bnho', att, hp).reshape(bsz, F, D)
            gnn_feat = jax.nn.elu(h_new + x)
            z = gnn_feat.mean(-1)
            w = jax.nn.sigmoid(jax.nn.relu(z @ se_w1 + se_b1) @ se_w2 + se_b2)
            s = gnn_feat * w[..., None]
            vid = jnp.einsum('bfd,fde->bfe', s[:, :F - 1], bi_W)
            p = jnp.stack([vid[:, i] * s[:, j] for i in range(F - 1) for j in range(i + 1, F)], axis=1)
            c = jnp.concatenate([gnn_feat.reshape(bsz, -1), p.reshape(bsz, -1)], axis=1)
            bn = lambda t, g_, b_: t * (g_ / jnp.sqrt(1.0 + eps)) + b_
            h1 = jax.nn.gelu(bn(c @ mlp_w1 + mlp_b1, bn1_g, bn1_b), approximate=False)
            h2 = jax.nn.gelu(bn(h1 @ mlp_w2 + mlp_b2, bn2_g, bn2_b), approximate=False)
            out = jax.nn.sigmoid(h2 @ mlp_w3 + mlp_b3)
            return out.squeeze(-1)
        key = jax.random.key(seed)
        ks = jax.random.split(key, 32)
        inp = {}
        inp['item_id'] = jax.random.randint(ks[0], (B,), 0, V)
        inp['item_mm'] = jax.random.normal(ks[1], (B, D), dtype=jnp.float32)
        inp['likes'] = jax.random.randint(ks[2], (B,), 0, C)
        inp['views'] = jax.random.randint(ks[3], (B,), 0, C)
        inp['item_seq'] = jax.random.randint(ks[4], (B, L), 0, V)
        g = lambda k, shape, s: jax.random.normal(k, shape, dtype=jnp.float32) * s
        inp['item_emb'] = g(ks[5], (V, D), 0.02).at[0].set(0.0)
        inp['cate_emb'] = g(ks[6], (C, D), 0.02)
        inp['mm_w'] = g(ks[7], (D, D), (2.0 / D) ** 0.5)
        inp['mm_b'] = jnp.zeros((D,), jnp.float32)
        inp['ln_g'] = jnp.ones((D,), jnp.float32)
        inp['ln_b'] = jnp.zeros((D,), jnp.float32)
        inp['gnn_W'] = g(ks[8], (H, D, HD), (2.0 / (D + HD)) ** 0.5 * 1.414)
        inp['gnn_a'] = g(ks[9], (H, 2 * HD, 1), 0.1)
        inp['se_w1'] = g(ks[10], (F, F // 2), 0.4)
        inp['se_b1'] = jnp.zeros((F // 2,), jnp.float32)
        inp['se_w2'] = g(ks[11], (F // 2, F), 0.4)
        inp['se_b2'] = jnp.zeros((F,), jnp.float32)
        inp['bi_W'] = g(ks[12], (F - 1, D, D), (2.0 / (2 * D)) ** 0.5)
        inp['mlp_w1'] = g(ks[13], (CIN, 512), (2.0 / CIN) ** 0.5)
        inp['mlp_b1'] = jnp.zeros((512,), jnp.float32)
        inp['bn1_g'] = jnp.ones((512,), jnp.float32)
        inp['bn1_b'] = jnp.zeros((512,), jnp.float32)
        inp['mlp_w2'] = g(ks[14], (512, 256), (2.0 / 512) ** 0.5)
        inp['mlp_b2'] = jnp.zeros((256,), jnp.float32)
        inp['bn2_g'] = jnp.ones((256,), jnp.float32)
        inp['bn2_b'] = jnp.zeros((256,), jnp.float32)
        inp['mlp_w3'] = g(ks[15], (256, 1), (2.0 / 256) ** 0.5)
        inp['mlp_b3'] = jnp.zeros((1,), jnp.float32)
        return inp
    _L0_rec_all = _L0_rec_setup()
    _L0_rec_in = {k: v for k, v in _L0_rec_all.items() if k in ('item_emb', 'cate_emb', 'mm_w', 'mm_b', 'ln_g', 'ln_b', 'gnn_W', 'gnn_a', 'se_w1', 'se_b1', 'se_w2', 'se_b2', 'bi_W', 'mlp_w1', 'mlp_b1', 'bn1_g', 'bn1_b', 'mlp_w2', 'mlp_b2', 'bn2_g', 'bn2_b', 'mlp_w3', 'mlp_b3', )}
    del _L0_rec_all

    return {
        "r_item_mm": r_item_mm,
        "r_item_id": r_item_id,
        "r_likes": r_likes,
        "r_views": r_views,
        "r_item_seq": r_item_seq,
        "L0_rec_item_emb": _L0_rec_in["item_emb"],
        "L0_rec_cate_emb": _L0_rec_in["cate_emb"],
        "L0_rec_mm_w": _L0_rec_in["mm_w"],
        "L0_rec_mm_b": _L0_rec_in["mm_b"],
        "L0_rec_ln_g": _L0_rec_in["ln_g"],
        "L0_rec_ln_b": _L0_rec_in["ln_b"],
        "L0_rec_gnn_W": _L0_rec_in["gnn_W"],
        "L0_rec_gnn_a": _L0_rec_in["gnn_a"],
        "L0_rec_se_w1": _L0_rec_in["se_w1"],
        "L0_rec_se_b1": _L0_rec_in["se_b1"],
        "L0_rec_se_w2": _L0_rec_in["se_w2"],
        "L0_rec_se_b2": _L0_rec_in["se_b2"],
        "L0_rec_bi_W": _L0_rec_in["bi_W"],
        "L0_rec_mlp_w1": _L0_rec_in["mlp_w1"],
        "L0_rec_mlp_b1": _L0_rec_in["mlp_b1"],
        "L0_rec_bn1_g": _L0_rec_in["bn1_g"],
        "L0_rec_bn1_b": _L0_rec_in["bn1_b"],
        "L0_rec_mlp_w2": _L0_rec_in["mlp_w2"],
        "L0_rec_mlp_b2": _L0_rec_in["mlp_b2"],
        "L0_rec_bn2_g": _L0_rec_in["bn2_g"],
        "L0_rec_bn2_b": _L0_rec_in["bn2_b"],
        "L0_rec_mlp_w3": _L0_rec_in["mlp_w3"],
        "L0_rec_mlp_b3": _L0_rec_in["mlp_b3"],
    }

def reference(r_item_mm, r_item_id, r_likes, r_views, r_item_seq, L0_rec_item_emb, L0_rec_cate_emb, L0_rec_mm_w, L0_rec_mm_b, L0_rec_ln_g, L0_rec_ln_b, L0_rec_gnn_W, L0_rec_gnn_a, L0_rec_se_w1, L0_rec_se_b1, L0_rec_se_w2, L0_rec_se_b2, L0_rec_bi_W, L0_rec_mlp_w1, L0_rec_mlp_b1, L0_rec_bn1_g, L0_rec_bn1_b, L0_rec_mlp_w2, L0_rec_mlp_b2, L0_rec_bn2_g, L0_rec_bn2_b, L0_rec_mlp_w3, L0_rec_mlp_b3):
    import jax
    import jax.numpy as jnp
    def _L0_rec_ref(item_id, item_mm, likes, views, item_seq, item_emb, cate_emb, mm_w, mm_b, ln_g, ln_b, gnn_W, gnn_a, se_w1, se_b1, se_w2, se_b2, bi_W, mlp_w1, mlp_b1, bn1_g, bn1_b, mlp_w2, mlp_b2, bn2_g, bn2_b, mlp_w3, mlp_b3):
        import jax, jax.numpy as jnp
        import numpy as np
        B, L, D, V, C = (16384, 50, 128, 91718, 11)
        H, HD, F = (4, 32, 6)
        NP = F * (F - 1) // 2
        CIN = F * D + NP * D

        def _forward(item_id, item_mm, likes, views, item_seq, item_emb, cate_emb, mm_w, mm_b, ln_g, ln_b, gnn_W, gnn_a, se_w1, se_b1, se_w2, se_b2, bi_W, mlp_w1, mlp_b1, bn1_g, bn1_b, mlp_w2, mlp_b2, bn2_g, bn2_b, mlp_w3, mlp_b3):
            bsz = item_id.shape[0]
            eps = 1e-05
            user_feat = jnp.zeros((bsz, D), item_mm.dtype)
            like_feat = cate_emb[likes]
            view_feat = cate_emb[views]
            id_feat = item_emb[item_id]
            y = item_mm @ mm_w + mm_b
            mu = y.mean(-1, keepdims=True)
            var = y.var(-1, keepdims=True)
            y = (y - mu) * jax.lax.rsqrt(var + eps) * ln_g + ln_b
            img_feat = jax.nn.gelu(y, approximate=False)
            seq_emb = item_emb[item_seq]
            mask = item_seq == 0
            seq_emb = jnp.where(mask[..., None], 0.0, seq_emb)
            cnt = jnp.clip(jnp.sum((~mask).astype(seq_emb.dtype), axis=1, keepdims=True), 1.0)
            hist_feat = seq_emb.sum(1) / cnt
            x = jnp.stack([user_feat, like_feat, view_feat, id_feat, img_feat, hist_feat], axis=1)
            hp = jnp.einsum('bni,hio->bnho', x, gnn_W)
            a1 = gnn_a[:, :HD, 0]
            a2 = gnn_a[:, HD:, 0]
            ei = jnp.einsum('bnhd,hd->bhn', hp, a1)
            ej = jnp.einsum('bnhd,hd->bhn', hp, a2)
            e = ei[:, :, :, None] + ej[:, :, None, :]
            e = jnp.where(e > 0, e, 0.2 * e)
            att = jax.nn.softmax(e, axis=-1)
            h_new = jnp.einsum('bhnm,bmho->bnho', att, hp).reshape(bsz, F, D)
            gnn_feat = jax.nn.elu(h_new + x)
            z = gnn_feat.mean(-1)
            w = jax.nn.sigmoid(jax.nn.relu(z @ se_w1 + se_b1) @ se_w2 + se_b2)
            s = gnn_feat * w[..., None]
            vid = jnp.einsum('bfd,fde->bfe', s[:, :F - 1], bi_W)
            p = jnp.stack([vid[:, i] * s[:, j] for i in range(F - 1) for j in range(i + 1, F)], axis=1)
            c = jnp.concatenate([gnn_feat.reshape(bsz, -1), p.reshape(bsz, -1)], axis=1)
            bn = lambda t, g_, b_: t * (g_ / jnp.sqrt(1.0 + eps)) + b_
            h1 = jax.nn.gelu(bn(c @ mlp_w1 + mlp_b1, bn1_g, bn1_b), approximate=False)
            h2 = jax.nn.gelu(bn(h1 @ mlp_w2 + mlp_b2, bn2_g, bn2_b), approximate=False)
            out = jax.nn.sigmoid(h2 @ mlp_w3 + mlp_b3)
            return out.squeeze(-1)
        return _forward(item_id, item_mm, likes, views, item_seq, item_emb, cate_emb, mm_w, mm_b, ln_g, ln_b, gnn_W, gnn_a, se_w1, se_b1, se_w2, se_b2, bi_W, mlp_w1, mlp_b1, bn1_g, bn1_b, mlp_w2, mlp_b2, bn2_g, bn2_b, mlp_w3, mlp_b3)

    y = _L0_rec_ref(r_item_id, r_item_mm, r_likes, r_views, r_item_seq, L0_rec_item_emb, L0_rec_cate_emb, L0_rec_mm_w, L0_rec_mm_b, L0_rec_ln_g, L0_rec_ln_b, L0_rec_gnn_W, L0_rec_gnn_a, L0_rec_se_w1, L0_rec_se_b1, L0_rec_se_w2, L0_rec_se_b2, L0_rec_bi_W, L0_rec_mlp_w1, L0_rec_mlp_b1, L0_rec_bn1_g, L0_rec_bn1_b, L0_rec_mlp_w2, L0_rec_mlp_b2, L0_rec_bn2_g, L0_rec_bn2_b, L0_rec_mlp_w3, L0_rec_mlp_b3)
    return y


_drawn_inputs = setup_inputs


def setup_inputs(seed=0):
    import zlib

    import numpy as np

    out = dict(_drawn_inputs(seed))
    spreads = {'L0_rec_mm_b': (0.0, 0.8),
     'L0_rec_ln_g': (1.0, 0.6),
     'L0_rec_ln_b': (0.0, 0.8),
     'L0_rec_se_b1': (0.0, 0.8),
     'L0_rec_se_b2': (0.0, 0.8),
     'L0_rec_mlp_b1': (0.0, 0.489),
     'L0_rec_bn1_g': (1.0, 0.6),
     'L0_rec_bn1_b': (0.0, 0.299),
     'L0_rec_mlp_b2': (0.0, 0.42),
     'L0_rec_bn2_g': (1.0, 0.6),
     'L0_rec_bn2_b': (0.0, 0.724)}
    factors = {'L0_rec_item_emb': 8.0,
     'L0_rec_cate_emb': 8.0,
     'L0_rec_se_w1': 8.0,
     'L0_rec_se_w2': 8.0,
     'L0_rec_bi_W': 5.194}
    for name, (base, spread) in spreads.items():
        noise = np.random.default_rng([zlib.crc32(name.encode()), seed]).standard_normal(out[name].shape)
        drawn = base * np.exp(spread * noise) if base else spread * noise
        out[name] = jnp.asarray(drawn.astype(out[name].dtype))
    for name, factor in factors.items():
        out[name] = (out[name] * factor).astype(out[name].dtype)
    return out
```

```python
from contextlib import ExitStack

import concourse.bass as bass
from concourse import mybir

P = 128
NODES = 6
HEADS = 4
FIRST_ROWS = 32
SLOTS = 2
LN_EPS = BN_EPS = 1e-5


def build_rec_head(nc, ids, item_mm, cates, item_emb, cate_emb, mm_w, mm_b, ln_g, ln_b, gnn_W, gnn_a,
                   se_w1, se_b1, se_w2, se_b2, bi_W, mlp_w1, mlp_b1, bn1_g, bn1_b, mlp_w2, mlp_b2,
                   bn2_g, bn2_b, mlp_w3, mlp_b3, out):
    fp32, int32 = mybir.dt.float32, mybir.dt.int32
    ALU, ACT, AX = mybir.AluOpType, mybir.ActivationFunctionType, mybir.AxisListType

    B, L = ids.shape[0], ids.shape[1] - 1
    ZERO_ROW = item_emb.shape[0] - 1
    D = item_emb.shape[1]
    CATES = cate_emb.shape[0]
    HD = D // HEADS
    TILES = B // P
    PAIRS = NODES * (NODES - 1) // 2
    KC = NODES + PAIRS
    H1, H2 = mlp_w1.shape[1], mlp_w2.shape[1]
    SE = se_w1.shape[1]
    REAL = NODES - 1
    SC = 2 * HEADS
    LAST = TILES // SLOTS - 1
    PAIR0 = [sum(NODES - 1 - a for a in range(i)) for i in range(NODES)]

    ctx = ExitStack()
    with ctx:
        def sb(name, shape, dt=fp32):
            return ctx.enter_context(nc.sbuf_tensor(name, shape, dt))

        def ps(name, width):
            return ctx.enter_context(nc.psum_tensor(name, [P, width], fp32))

        def sem(name):
            return ctx.enter_context(nc.semaphore(name))

        ident = sb("ident", [P, P])
        cate_no_i = sb("cate_no_i", [CATES, 1], int32)
        cate_no = sb("cate_no", [CATES, 1])
        cate_sb = sb("cate_sb", [CATES, D])
        mmw_sb = sb("mmw_sb", [P, D])
        mmb_bc = sb("mmb_bc", [P, D])
        lng_bc = sb("lng_bc", [P, D])
        lnb_bc = sb("lnb_bc", [P, D])
        gnn_sb = sb("gnn_sb", [P, HEADS, HD])
        a_bc = sb("a_bc", [P, HEADS, 2, HD])
        score_w = sb("score_w", [P, 2, HEADS])
        se1_raw = sb("se1_raw", [P, NODES, SE])
        se2_raw = sb("se2_raw", [P, SE, NODES])
        se1_w = sb("se1_w", [P, SE, NODES + 1])
        se2_w = sb("se2_w", [P, NODES, SE + 1])
        bi_sb = sb("bi_sb", [P, REAL, D])
        w1_sb = sb("w1_sb", [P, KC, H1])
        w2_sb = sb("w2_sb", [P, H1 // P, H2])
        bn1g_bc = sb("bn1g_bc", [P, H1])
        bias1_bc = sb("bias1_bc", [P, H1])
        bn2g_bc = sb("bn2g_bc", [P, H2])
        bias2_bc = sb("bias2_bc", [P, H2])
        w3_bc = sb("w3_bc", [P, H2])
        b3_bc = sb("b3_bc", [P, 1])

        ids_raw = sb("ids_raw", [P, SLOTS, L + 1], int32)
        ids_use = sb("ids_use", [P, SLOTS, L + 1], int32)
        is_pad = sb("is_pad", [P, SLOTS, L])
        count = sb("count", [P, SLOTS, 1])
        inv_count = sb("inv_count", [P, SLOTS, 1])
        mm_sb = sb("mm_sb", [P, SLOTS, D])
        cates_sb = sb("cates_sb", [CATES, SLOTS, 2, P], int32)
        rows = sb("rows", [P, SLOTS, L + 1, D])

        onehot = sb("onehot", [CATES, 2, P])
        mmT = sb("mmT", [P, P])
        ln_stats = sb("ln_stats", [P, 6])
        ln_mv = sb("ln_mv", [P, 2])
        ln_eps = sb("ln_eps", [P, 1])
        ln_std = sb("ln_std", [P, 1])
        ln_rstd = sb("ln_rstd", [P, 1])
        img_pre = sb("img_pre", [P, D])
        hist_sum = sb("hist_sum", [P, D])
        mix = sb("mix", [P, SLOTS, NODES, NODES, D])
        xT = sb("xT", [P, REAL, P])
        scores = sb("scores", [P, NODES, SC])
        e = sb("e", [P, NODES, NODES, HEADS])
        e_max = sb("e_max", [P, NODES, HEADS])
        att = sb("att", [P, NODES, NODES, HEADS])
        att_sum = sb("att_sum", [P, NODES, HEADS])
        att_inv = sb("att_inv", [P, NODES, HEADS])
        v = sb("v", [P, NODES, D])
        elu_e = sb("elu_e", [P, NODES, D])
        g = sb("g", [P, NODES, D])
        z = sb("z", [P, 1, NODES + 1])
        se_p1 = sb("se_p1", [P, SE, NODES + 1])
        se_h = sb("se_h", [P, 1, SE + 1])
        se_p2 = sb("se_p2", [P, NODES, SE + 1])
        se_a = sb("se_a", [P, NODES])
        se_e = sb("se_e", [P, NODES])
        se_d = sb("se_d", [P, NODES])
        gate = sb("gate", [P, NODES, 1])
        s = sb("s", [P, NODES, D])
        gT = sb("gT", [P, NODES, P])
        sT = sb("sT", [P, NODES, P])
        pairT = sb("pairT", [P, PAIRS, P])
        h1 = sb("h1", [P, H1])
        h1T = sb("h1T", [P, H1 // P, P])
        h2 = sb("h2", [P, H2])
        logits = sb("logits", [P, TILES])
        probs = sb("probs", [P, TILES])
        outT = sb("outT", [TILES, P])

        ps_front = ps("ps_front", 512)
        ps_cate = ps("ps_cate", 512)
        ps_x = ps("ps_x", 512)
        ps_hp = ps("ps_hp", 1024)
        ps_gs = ps("ps_gs", 1536)
        ps_y = ps_front[:, D:2 * D]
        ps_h2 = ps_gs[:, 1024:1024 + H2]
        ps_h1 = ps_x[:, 0:H1]
        ps_sc = ps_hp[:, REAL * D:REAL * D + REAL * SC]

        ids_loaded = [sem(f"ids_loaded{j}") for j in range(SLOTS)]
        mm_loaded = [sem(f"mm_loaded{j}") for j in range(SLOTS)]
        cates_loaded = [sem(f"cates_loaded{j}") for j in range(SLOTS)]
        id_row_landed = [sem(f"id_row_landed{j}") for j in range(SLOTS)]
        rows_a_landed = [sem(f"rows_a_landed{j}") for j in range(SLOTS)]
        rows_b_landed = [sem(f"rows_b_landed{j}") for j in range(SLOTS)]
        gathers_begun = sem("gathers_begun")
        loads_begun = sem("loads_begun")
        small_loaded = sem("small_loaded")
        w1_loaded = sem("w1_loaded")
        out_stored = sem("out_stored")
        zeros_made = sem("zeros_made")
        ident_made = sem("ident_made")
        cate_no_made = sem("cate_no_made")
        prep_step = sem("prep_step")
        weights_ready = sem("weights_ready")
        pad_known = sem("pad_known")
        pad_counted = sem("pad_counted")
        count_ready = sem("count_ready")
        ids_ready = sem("ids_ready")
        onehot_ready = sem("onehot_ready")
        mmT_ready = sem("mmT_ready")
        mmT_copied = sem("mmT_copied")
        y_ready = sem("y_ready")
        stats_ready = sem("stats_ready")
        meanvar_ready = sem("meanvar_ready")
        std_ready = sem("std_ready")
        rstd_ready = sem("rstd_ready")
        centred = sem("centred")
        scaled = sem("scaled")
        img_pre_ready = sem("img_pre_ready")
        img_ready = sem("img_ready")
        cate_rows_ready = sem("cate_rows_ready")
        cate_rows_copied = sem("cate_rows_copied")
        idimgT_ready = sem("idimgT_ready")
        idimgT_copied = sem("idimgT_copied")
        rows_a_summed = sem("rows_a_summed")
        rows_summed = sem("rows_summed")
        hist_ready = sem("hist_ready")
        histT_ready = sem("histT_ready")
        histT_copied = sem("histT_copied")
        hp_ready = sem("hp_ready")
        scores_copied = sem("scores_copied")
        e_summed = sem("e_summed")
        e_leaky = sem("e_leaky")
        e_max_ready = sem("e_max_ready")
        e_shifted = sem("e_shifted")
        att_exp_ready = sem("att_exp_ready")
        att_summed = sem("att_summed")
        att_inv_ready = sem("att_inv_ready")
        att_ready = sem("att_ready")
        mixed = sem("mixed")
        v_ready = sem("v_ready")
        negpart_ready = sem("negpart_ready")
        elu_exp_ready = sem("elu_exp_ready")
        g_ready = sem("g_ready")
        z_ready = sem("z_ready")
        se_p1_ready = sem("se_p1_ready")
        se_h_ready = sem("se_h_ready")
        se_p2_ready = sem("se_p2_ready")
        se_a_ready = sem("se_a_ready")
        se_e_ready = sem("se_e_ready")
        se_d_ready = sem("se_d_ready")
        gate_ready = sem("gate_ready")
        s_ready = sem("s_ready")
        gT_ready = sem("gT_ready")
        gT_copied = sem("gT_copied")
        sT_ready = sem("sT_ready")
        sT_copied = sem("sT_copied")
        bilinear_ready = sem("bilinear_ready")
        pairs_ready = [sem(f"pairs_ready{i}") for i in range(REAL)]
        h1_pre_ready = sem("h1_pre_ready")
        h1_ready = sem("h1_ready")
        h1T_ready = sem("h1T_ready")
        h1T_copied = sem("h1T_copied")
        h2_pre_ready = sem("h2_pre_ready")
        h2_ready = sem("h2_ready")
        h2_weighted = sem("h2_weighted")
        logits_ready = sem("logits_ready")
        probs_ready = sem("probs_ready")
        probsT_ready = sem("probsT_ready")
        outT_ready = sem("outT_ready")

        def value(eng, x):
            return x if isinstance(x, int) else eng.snap(x)

        def over_tiles(eng, tile):
            with eng.Fori(0, LAST) as i:
                for j in range(SLOTS):
                    tile(i, j, False)
            for j in range(SLOTS):
                tile(LAST, j, True)

        small_loads = [
            (cate_sb[:], cate_emb),
            (mmw_sb[:], mm_w),
            (mmb_bc[:], mm_b.partition_broadcast(P)),
            (lng_bc[:], ln_g.partition_broadcast(P)),
            (lnb_bc[:], ln_b.partition_broadcast(P)),
            (gnn_sb[:], gnn_W.rearrange("h i o -> i h o")),
            (a_bc[:].rearrange("p h t o -> p (h t o)"),
             gnn_a.rearrange("h t one -> (h t one)").partition_broadcast(P)),
            (se1_raw[:].rearrange("p n k -> p (n k)"), se_w1.rearrange("n k -> (n k)").partition_broadcast(P)),
            (se2_raw[:].rearrange("p k n -> p (k n)"), se_w2.rearrange("k n -> (k n)").partition_broadcast(P)),
            (z[:, 0, 0:SE], se_b1.partition_broadcast(P)),
            (se_a[:], se_b2.partition_broadcast(P)),
            (bi_sb[:], bi_W.rearrange("n d e -> d n e")),
            (w2_sb[:], mlp_w2.rearrange("(k p) n -> p k n", p=P)),
            (bn1g_bc[:], bn1_g.partition_broadcast(P)),
            (bias1_bc[:], mlp_b1.partition_broadcast(P)),
            (h1[:], bn1_b.partition_broadcast(P)),
            (bn2g_bc[:], bn2_g.partition_broadcast(P)),
            (bias2_bc[:], mlp_b2.partition_broadcast(P)),
            (h2[:], bn2_b.partition_broadcast(P)),
            (w3_bc[:], mlp_w3.rearrange("k one -> (k one)").partition_broadcast(P)),
            (b3_bc[:], mlp_b3.partition_broadcast(P)),
        ]

        block = ctx.enter_context(nc.Block())

        @block.sync
        def _(sp):
            def load_ids(row, j):
                sp.dma_start(ids_raw[:, j, :], ids[bass.ds(row, P), :]).then_inc(ids_loaded[j], 16)

            def load_mm(row, j):
                sp.dma_start(mm_sb[:, j, :], item_mm[bass.ds(row, P), :]).then_inc(mm_loaded[j], 16)

            def load_cates(row, j):
                sp.dma_start(cates_sb[:, j, :, :],
                             cates[:, bass.ds(row, P)].partition_broadcast(CATES)).then_inc(cates_loaded[j], 16)

            for j in range(SLOTS):
                load_ids(j * P, j)
            for j in range(SLOTS):
                load_mm(j * P, j)
                load_cates(j * P, j)

            with sp.Fori(0, LAST) as i:
                for j in range(SLOTS):
                    n = value(sp, SLOTS * i + j + 1)
                    row = value(sp, (SLOTS * (i + 1) + j) * P)
                    sp.wait_ge(ids_ready, n)
                    sp.sem_inc(loads_begun, 1)
                    load_ids(row, j)
                    sp.wait_ge(mmT_ready, n)
                    sp.sem_inc(loads_begun, 1)
                    load_mm(row, j)
                    sp.wait_ge(onehot_ready, n)
                    sp.sem_inc(loads_begun, 1)
                    load_cates(row, j)
            sp.wait_ge(outT_ready, 1)
            sp.dma_start(out.rearrange("(t p) -> t p", p=P), outT[:]).then_inc(out_stored, 16)
            sp.wait_ge(out_stored, 16)

        @block.gpsimd
        def _(pool):
            nc.gpsimd.memset(ident[:], 0.0).then_inc(zeros_made, 1)
            pool.wait_ge(zeros_made, 1)
            nc.gpsimd.affine_select(out=ident[:], in_=ident[:], compare_op=ALU.not_equal, fill=1.0, base=0,
                                    pattern=[[-1, P]], channel_multiplier=1).then_inc(ident_made, 1)
            nc.gpsimd.iota(cate_no_i[:], pattern=[[0, 1]], base=0, channel_multiplier=1).then_inc(cate_no_made, 1)

            def gather(dst, j, column):
                return nc.gpsimd.indirect_dma_start(
                    out=dst, out_offset=None, in_=item_emb,
                    in_offset=bass.IndirectOffsetOnAxis(ap=ids_use[:, j, column:column + 1], axis=0))

            def tile(i, j, last):
                pool.wait_ge(ids_ready, value(pool, SLOTS * i + j + 1))
                pool.sem_inc(gathers_begun, 1)
                gather(mix[:, j, 3, 0, :], j, 0).then_inc(id_row_landed[j], 16)
                for k in range(FIRST_ROWS):
                    gather(rows[:, j, k, :], j, 1 + k).then_inc(rows_a_landed[j], 16)
                for k in range(FIRST_ROWS, L):
                    gather(rows[:, j, k, :], j, 1 + k).then_inc(rows_b_landed[j], 16)

            over_tiles(pool, tile)

        @block.scalar
        def _(act):
            for dst, src in small_loads:
                act.dma_start(dst, src).then_inc(small_loaded, 16)
            act.dma_start(w1_sb[:], mlp_w1.rearrange("(k p) n -> p k n", p=P)).then_inc(w1_loaded, 16)
            act.wait_ge(weights_ready, 1)

            def tile(i, j, last):
                n = value(act, SLOTS * i + j + 1)
                act.wait_ge(mmT_ready, n)
                nc.scalar.copy(mmT[:], ps_front[:, 0:P]).then_inc(mmT_copied, 1)
                act.wait_ge(cate_rows_ready, n)
                nc.scalar.copy(mix[:, j, 1:3, 0, :], ps_cate[:, 0:2 * D].rearrange("p (n d) -> p n d", n=2))
                nc.scalar.copy(xT[:, 0:2, :], ps_cate[:, 2 * D:4 * D].rearrange("p (n d) -> p n d", n=2)
                               ).then_inc(cate_rows_copied, 1)
                act.wait_ge(meanvar_ready, n)
                nc.scalar.activation(ln_std[:], ln_mv[:, 1:2], ACT.Sqrt, bias=ln_eps[:, 0:1]).then_inc(std_ready, 1)
                act.wait_ge(img_pre_ready, n)
                nc.scalar.activation(mix[:, j, 4, 0, :], img_pre[:], ACT.Gelu).then_inc(img_ready, 1)
                act.wait_ge(idimgT_ready, n)
                nc.scalar.copy(xT[:, 2:4, :], ps_x[:, 0:2 * P].rearrange("p (n s) -> p n s", n=2)
                               ).then_inc(idimgT_copied, 1)
                act.wait_ge(histT_ready, n)
                nc.scalar.copy(xT[:, 4, :], ps_x[:, 2 * P:3 * P]).then_inc(histT_copied, 1)
                act.wait_ge(e_shifted, n)
                nc.scalar.activation(att[:], e[:], ACT.Exp).then_inc(att_exp_ready, 1)
                act.wait_ge(v_ready, n)
                nc.scalar.activation(elu_e[:], v[:], ACT.Relu, scale=-1.0).then_inc(negpart_ready, 1)
                act.wait_ge(negpart_ready, n)
                nc.scalar.activation(elu_e[:], elu_e[:], ACT.Exp, scale=-1.0).then_inc(elu_exp_ready, 1)
                act.wait_ge(gT_ready, n)
                nc.scalar.copy(gT[:].rearrange("p n s -> p (n s)"), ps_gs[:, 0:NODES * P]).then_inc(gT_copied, 1)
                act.wait_ge(se_a_ready, n)
                nc.scalar.activation(se_e[:], se_a[:], ACT.Exp, scale=-1.0).then_inc(se_e_ready, 1)
                act.wait_ge(h1_pre_ready, n)
                nc.scalar.activation(h1[:], ps_h1, ACT.Gelu).then_inc(h1_ready, 1)
                act.wait_ge(h2_pre_ready, n)
                nc.scalar.activation(h2[:], ps_h2, ACT.Gelu).then_inc(h2_ready, 1)

            over_tiles(act, tile)
            act.wait_ge(logits_ready, TILES)
            nc.scalar.activation(probs[:], logits[:], ACT.Sigmoid, bias=b3_bc[:, 0:1]).then_inc(probs_ready, 1)
            act.wait_ge(probsT_ready, 1)
            nc.scalar.copy(outT[:], ps_front[0:TILES, 0:P]).then_inc(outT_ready, 1)

        @block.vector
        def _(dve):
            def make_ids(n, count_loaded, j):
                dve.wait_ge(ids_loaded[j], count_loaded)
                nc.vector.tensor_scalar(is_pad[:, j, :], ids_raw[:, j, 1:L + 1], 0.0, None, ALU.is_equal
                                        ).then_inc(pad_known, 1)
                nc.vector.tensor_copy(ids_use[:, j, 0:1], ids_raw[:, j, 0:1])
                dve.wait_ge(pad_known, n)
                nc.vector.tensor_reduce(count[:, j, :], is_pad[:, j, :], AX.X, ALU.add, negate=True
                                        ).then_inc(pad_counted, 1)
                nc.vector.scalar_tensor_tensor(ids_use[:, j, 1:L + 1], is_pad[:, j, :], float(ZERO_ROW),
                                               ids_raw[:, j, 1:L + 1], ALU.mult, ALU.add)
                dve.wait_ge(pad_counted, n)
                nc.vector.tensor_scalar(count[:, j, :], count[:, j, :], float(L), 1.0, ALU.add, ALU.max
                                        ).then_inc(count_ready, 1)
                dve.wait_ge(count_ready, n)
                nc.vector.reciprocal(inv_count[:, j, :], count[:, j, :]).then_inc(ids_ready, 1)

            for j in range(SLOTS):
                make_ids(j + 1, 16, j)

            nc.vector.memset(mix[:, :, 0, 0, :], 0.0)
            nc.vector.memset(scores[:, 0, :], 0.0)
            nc.vector.memset(se_h[:], 1.0)
            nc.vector.memset(ln_eps[:], LN_EPS)
            dve.wait_ge(cate_no_made, 1)
            nc.vector.tensor_copy(cate_no[:], cate_no_i[:])
            dve.wait_ge(small_loaded, 16 * len(small_loads))
            scale = float(1.0 / (1.0 + BN_EPS) ** 0.5)
            nc.vector.tensor_scalar(bn1g_bc[:], bn1g_bc[:], scale, None, ALU.mult)
            nc.vector.tensor_scalar(bn2g_bc[:], bn2g_bc[:], scale, None, ALU.mult)
            nc.vector.tensor_scalar(se1_w[:, :, 0:NODES], se1_raw[:].rearrange("p n k -> p k n"), 1.0 / D, None,
                                    ALU.mult)
            nc.vector.tensor_copy(se1_w[:, :, NODES], z[:, 0, 0:SE])
            nc.vector.tensor_copy(se2_w[:, :, 0:SE], se2_raw[:].rearrange("p k n -> p n k"))
            nc.vector.tensor_copy(se2_w[:, :, SE], se_a[:])
            for t in range(2):
                nc.vector.tensor_tensor(v[:, t, :].rearrange("p (h o) -> p h o", h=HEADS), gnn_sb[:], a_bc[:, :, t, :],
                                        ALU.mult).then_inc(prep_step, 1)
            dve.wait_ge(prep_step, 2)
            nc.vector.memset(z[:], 1.0)
            for t in range(2):
                nc.vector.tensor_reduce(score_w[:, t, :], v[:, t, :].rearrange("p (h o) -> p h o", h=HEADS), AX.X,
                                        ALU.add)
            nc.vector.tensor_tensor(bias1_bc[:], bias1_bc[:], bn1g_bc[:], ALU.mult).then_inc(prep_step, 1)
            nc.vector.tensor_tensor(bias2_bc[:], bias2_bc[:], bn2g_bc[:], ALU.mult).then_inc(prep_step, 1)
            dve.wait_ge(prep_step, 4)
            nc.vector.tensor_tensor(bias1_bc[:], bias1_bc[:], h1[:], ALU.add)
            nc.vector.tensor_tensor(bias2_bc[:], bias2_bc[:], h2[:], ALU.add)
            nc.vector.tensor_tensor(w2_sb[:], w2_sb[:], bn2g_bc[:].unsqueeze(1).to_broadcast([P, H1 // P, H2]),
                                    ALU.mult)
            dve.wait_ge(w1_loaded, 16)
            nc.vector.tensor_tensor(w1_sb[:], w1_sb[:], bn1g_bc[:].unsqueeze(1).to_broadcast([P, KC, H1]),
                                    ALU.mult).then_inc(weights_ready, 1)

            def tile(i, j, last):
                n = value(dve, SLOTS * i + j + 1)
                loaded = value(dve, 16 * (i + 1))
                dve.wait_ge(y_ready, n)
                nc.vector.bn_stats(ln_stats[:], ps_y).then_inc(stats_ready, 1)
                dve.wait_ge(cates_loaded[j], loaded)
                dve.wait_ge(stats_ready, n)
                nc.vector.tensor_scalar(onehot[:], cates_sb[:, j, :, :], cate_no[:, 0:1], None, ALU.is_equal
                                        ).then_inc(onehot_ready, 1)
                nc.vector.bn_aggr(ln_mv[:], ln_stats[:]).then_inc(meanvar_ready, 1)
                dve.wait_ge(std_ready, n)
                nc.vector.reciprocal(ln_rstd[:], ln_std[:]).then_inc(rstd_ready, 1)
                dve.wait_ge(rstd_ready, n)
                nc.vector.tensor_scalar(img_pre[:], ps_y, ln_mv[:, 0:1], ln_rstd[:, 0:1], ALU.subtract, ALU.mult
                                        ).then_inc(centred, 1)
                dve.wait_ge(centred, n)
                nc.vector.tensor_tensor(img_pre[:], img_pre[:], lng_bc[:], ALU.mult).then_inc(scaled, 1)
                dve.wait_ge(scaled, n)
                nc.vector.tensor_tensor(img_pre[:], img_pre[:], lnb_bc[:], ALU.add).then_inc(img_pre_ready, 1)

                dve.wait_ge(rows_a_landed[j], value(dve, 16 * FIRST_ROWS * (i + 1)))
                nc.vector.tensor_reduce(rows[:, j, L, :], rows[:, j, 0:FIRST_ROWS, :].rearrange("p l d -> p d l"),
                                        AX.X, ALU.add).then_inc(rows_a_summed, 1)
                dve.wait_ge(rows_b_landed[j], value(dve, 16 * (L - FIRST_ROWS) * (i + 1)))
                dve.wait_ge(rows_a_summed, n)
                nc.vector.tensor_reduce(hist_sum[:], rows[:, j, FIRST_ROWS:L + 1, :].rearrange("p l d -> p d l"),
                                        AX.X, ALU.add).then_inc(rows_summed, 1)
                dve.wait_ge(rows_summed, n)
                nc.vector.tensor_scalar(mix[:, j, 5, 0, :], hist_sum[:], inv_count[:, j, 0:1], None, ALU.mult
                                        ).then_inc(hist_ready, 1)

                dve.wait_ge(hp_ready, n)
                nc.vector.tensor_copy(scores[:, 1:NODES, :], ps_sc.rearrange("p (n c) -> p n c", c=SC)
                                      ).then_inc(scores_copied, 1)
                dve.wait_ge(scores_copied, n)
                nc.vector.tensor_tensor(
                    e[:], scores[:, :, 0:HEADS].unsqueeze(2).to_broadcast([P, NODES, NODES, HEADS]),
                    scores[:, :, HEADS:SC].unsqueeze(1).to_broadcast([P, NODES, NODES, HEADS]), ALU.add
                ).then_inc(e_summed, 1)
                dve.wait_ge(e_summed, n)
                nc.vector.scalar_tensor_tensor(e[:], e[:], 0.2, e[:], ALU.mult, ALU.max).then_inc(e_leaky, 1)
                dve.wait_ge(e_leaky, n)
                nc.vector.tensor_reduce(e_max[:], e[:].rearrange("p n m h -> p n h m"), AX.X, ALU.max
                                        ).then_inc(e_max_ready, 1)
                dve.wait_ge(e_max_ready, n)
                nc.vector.tensor_tensor(e[:], e[:], e_max[:].unsqueeze(2).to_broadcast([P, NODES, NODES, HEADS]),
                                        ALU.subtract).then_inc(e_shifted, 1)
                dve.wait_ge(att_exp_ready, n)
                nc.vector.tensor_reduce(att_sum[:], att[:].rearrange("p n m h -> p n h m"), AX.X, ALU.add
                                        ).then_inc(att_summed, 1)
                dve.wait_ge(att_summed, n)
                nc.vector.reciprocal(att_inv[:], att_sum[:]).then_inc(att_inv_ready, 1)
                dve.wait_ge(att_inv_ready, n)
                nc.vector.tensor_tensor(att[:], att[:], att_inv[:].unsqueeze(2).to_broadcast([P, NODES, NODES, HEADS]),
                                        ALU.mult).then_inc(att_ready, 1)

                dve.wait_ge(att_ready, n)
                nc.vector.tensor_tensor(
                    mix[:, j, :, 1:NODES, :].rearrange("p n m (h o) -> p n (m h) o", h=HEADS),
                    att[:, :, 1:NODES, :].rearrange("p n m h -> p n (m h)").unsqueeze(3).to_broadcast(
                        [P, NODES, REAL * HEADS, HD]),
                    ps_hp[:, 0:REAL * D].rearrange("p (a o) -> p a o", o=HD).unsqueeze(1).to_broadcast(
                        [P, NODES, REAL * HEADS, HD]), ALU.mult).then_inc(mixed, 1)
                dve.wait_ge(mixed, n)
                nc.vector.tensor_reduce(v[:], mix[:, j, :, :, :].rearrange("p n m d -> p n d m"), AX.X, ALU.add
                                        ).then_inc(v_ready, 1)

                if not last:
                    dve.wait_ge(v_ready, n)
                    make_ids(value(dve, SLOTS * (i + 1) + j + 1), value(dve, 16 * (i + 2)), j)

                dve.wait_ge(elu_exp_ready, n)
                nc.vector.scalar_tensor_tensor(g[:], elu_e[:], -1.0, v[:], ALU.add, ALU.max).then_inc(g_ready, 1)

                dve.wait_ge(g_ready, n)
                nc.vector.tensor_reduce(z[:, 0, 0:NODES], g[:], AX.X, ALU.add).then_inc(z_ready, 1)
                dve.wait_ge(z_ready, n)
                nc.vector.tensor_tensor(se_p1[:], z[:].to_broadcast([P, SE, NODES + 1]), se1_w[:], ALU.mult
                                        ).then_inc(se_p1_ready, 1)
                dve.wait_ge(se_p1_ready, n)
                nc.vector.tensor_reduce(se_h[:, 0, 0:SE], se_p1[:], AX.X, ALU.add).then_inc(se_h_ready, 1)
                dve.wait_ge(se_h_ready, n)
                nc.vector.scalar_tensor_tensor(se_p2[:], se_h[:].to_broadcast([P, NODES, SE + 1]), 0.0, se2_w[:],
                                               ALU.max, ALU.mult).then_inc(se_p2_ready, 1)
                dve.wait_ge(se_p2_ready, n)
                nc.vector.tensor_reduce(se_a[:], se_p2[:], AX.X, ALU.add).then_inc(se_a_ready, 1)
                dve.wait_ge(se_e_ready, n)
                nc.vector.tensor_scalar(se_d[:], se_e[:], 1.0, None, ALU.add).then_inc(se_d_ready, 1)
                dve.wait_ge(se_d_ready, n)
                nc.vector.reciprocal(gate[:, :, 0], se_d[:]).then_inc(gate_ready, 1)
                dve.wait_ge(gate_ready, n)
                nc.vector.tensor_tensor(s[:], g[:], gate[:].to_broadcast([P, NODES, D]), ALU.mult
                                        ).then_inc(s_ready, 1)
                dve.wait_ge(sT_ready, n)
                nc.vector.tensor_copy(sT[:].rearrange("p n s -> p (n s)"), ps_gs[:, NODES * P:2 * NODES * P]
                                      ).then_inc(sT_copied, 1)

                dve.wait_ge(bilinear_ready, n)
                dve.wait_ge(sT_copied, n)
                for a in range(REAL):
                    others = NODES - 1 - a
                    nc.vector.tensor_tensor(
                        pairT[:, PAIR0[a]:PAIR0[a] + others, :],
                        ps_hp[:, a * P:(a + 1) * P].unsqueeze(1).to_broadcast([P, others, P]),
                        sT[:, a + 1:NODES, :], ALU.mult).then_inc(pairs_ready[a], 1)
                dve.wait_ge(h1T_ready, n)
                nc.vector.tensor_copy(h1T[:].rearrange("p k s -> p (k s)"), ps_gs[:, 0:H1]).then_inc(h1T_copied, 1)

                dve.wait_ge(h2_ready, n)
                nc.vector.tensor_tensor(h2[:], h2[:], w3_bc[:], ALU.mult).then_inc(h2_weighted, 1)
                dve.wait_ge(h2_weighted, n)
                t = value(dve, SLOTS * i + j)
                nc.vector.tensor_reduce(logits[:, bass.ds(t, 1)], h2[:], AX.X, ALU.add).then_inc(logits_ready, 1)

            over_tiles(dve, tile)

        @block.tensor
        def _(pe):
            pe.wait_ge(ident_made, 1)
            pe.wait_ge(weights_ready, 1)

            def tile(i, j, last):
                n = value(pe, SLOTS * i + j + 1)
                loaded = value(pe, 16 * (i + 1))
                pe.wait_ge(mm_loaded[j], loaded)
                nc.tensor.transpose(ps_front[:, 0:P], mm_sb[:, j, :], ident[:]).then_inc(mmT_ready, 1)
                pe.wait_ge(mmT_copied, n)
                nc.tensor.matmul(ps_y, ident[:], mmb_bc[:], start=True, stop=False)
                nc.tensor.matmul(ps_y, mmT[:], mmw_sb[:], start=False, stop=True).then_inc(y_ready, 1)
                pe.wait_ge(onehot_ready, n)
                for k in range(2):
                    nc.tensor.matmul(ps_cate[:, k * D:(k + 1) * D], onehot[:, k, :], cate_sb[:], start=True, stop=True)
                nc.tensor.matmul(ps_cate[:, 2 * D:4 * D], cate_sb[:], onehot[:].rearrange("c k s -> c (k s)"),
                                 start=True, stop=True).then_inc(cate_rows_ready, 1)
                pe.wait_ge(id_row_landed[j], loaded)
                nc.tensor.transpose(ps_x[:, 0:P], mix[:, j, 3, 0, :], ident[:])
                pe.wait_ge(img_ready, n)
                nc.tensor.transpose(ps_x[:, P:2 * P], mix[:, j, 4, 0, :], ident[:]).then_inc(idimgT_ready, 1)

                def project(m):
                    nc.tensor.matmul(ps_hp[:, m * D:(m + 1) * D], xT[:, m, :],
                                     gnn_sb[:].rearrange("p h o -> p (h o)"), start=True, stop=True)
                    return nc.tensor.matmul(ps_sc[:, m * SC:(m + 1) * SC], xT[:, m, :],
                                            score_w[:].rearrange("p t h -> p (t h)"), start=True, stop=True)

                pe.wait_ge(cate_rows_copied, n)
                pe.wait_ge(idimgT_copied, n)
                for m in range(REAL - 1):
                    project(m)
                pe.wait_ge(hist_ready, n)
                nc.tensor.transpose(ps_x[:, 2 * P:3 * P], mix[:, j, 5, 0, :], ident[:]).then_inc(histT_ready, 1)
                pe.wait_ge(histT_copied, n)
                project(REAL - 1).then_inc(hp_ready, 1)

                def layer1(lhsT, k, stop=False):
                    return nc.tensor.matmul(ps_h1, lhsT, w1_sb[:, k, :], start=False, stop=stop)

                nc.tensor.matmul(ps_h1, ident[:], bias1_bc[:], start=True, stop=False)
                pe.wait_ge(g_ready, n)
                for k in range(NODES):
                    step = nc.tensor.transpose(ps_gs[:, k * P:(k + 1) * P], g[:, k, :], ident[:])
                step.then_inc(gT_ready, 1)
                pe.wait_ge(gT_copied, n)
                for k in range(NODES // 2):
                    layer1(gT[:, k, :], k)
                pe.wait_ge(s_ready, n)
                for k in range(NODES):
                    step = nc.tensor.transpose(ps_gs[:, (NODES + k) * P:(NODES + k + 1) * P], s[:, k, :], ident[:])
                step.then_inc(sT_ready, 1)
                for k in range(NODES // 2, NODES):
                    layer1(gT[:, k, :], k)
                pe.wait_ge(sT_copied, n)
                for a in range(REAL):
                    step = nc.tensor.matmul(ps_hp[:, a * P:(a + 1) * P], bi_sb[:, a, :], sT[:, a, :],
                                            start=True, stop=True)
                step.then_inc(bilinear_ready, 1)
                for a in range(REAL):
                    pe.wait_ge(pairs_ready[a], n)
                    for k in range(PAIR0[a], PAIR0[a] + NODES - 1 - a):
                        step = layer1(pairT[:, k, :], NODES + k, stop=k == PAIRS - 1)
                step.then_inc(h1_pre_ready, 1)

                nc.tensor.matmul(ps_h2, ident[:], bias2_bc[:], start=True, stop=False)
                pe.wait_ge(h1_ready, n)
                for k in range(H1 // P):
                    step = nc.tensor.transpose(ps_gs[:, k * P:(k + 1) * P], h1[:, k * P:(k + 1) * P], ident[:])
                step.then_inc(h1T_ready, 1)
                pe.wait_ge(h1T_copied, n)
                for k in range(H1 // P):
                    step = nc.tensor.matmul(ps_h2, h1T[:, k, :], w2_sb[:, k, :], start=False, stop=k == H1 // P - 1)
                step.then_inc(h2_pre_ready, 1)

            over_tiles(pe, tile)
            pe.wait_ge(probs_ready, 1)
            nc.tensor.transpose(ps_front[0:TILES, 0:P], probs[:], ident[:]).then_inc(probsT_ready, 1)


_PLAIN = ["item_emb", "cate_emb", "mm_w", "mm_b", "ln_g", "ln_b", "gnn_W", "gnn_a", "se_w1", "se_b1", "se_w2",
          "se_b2", "bi_W", "mlp_w1", "mlp_b1", "bn1_g", "bn1_b", "mlp_w2", "mlp_b2", "bn2_g", "bn2_b", "mlp_w3",
          "mlp_b3"]


def kernel(**inputs):
    import numpy as np
    import concourse.bacc as bacc
    from concourse.bass_utils import run_bass_kernel_spmd

    item_id = np.asarray(inputs["r_item_id"])
    arrays = {
        "ids": np.concatenate([item_id[:, None], np.asarray(inputs["r_item_seq"])], axis=1),
        "item_mm": np.ascontiguousarray(inputs["r_item_mm"]),
        "cates": np.stack([np.asarray(inputs["r_likes"]), np.asarray(inputs["r_views"])]),
    }
    for name in _PLAIN:
        arrays[name] = np.ascontiguousarray(inputs[f"L0_rec_{name}"])
    table = arrays["item_emb"]
    arrays["item_emb"] = np.concatenate([table, np.zeros((1, table.shape[1]), table.dtype)])

    nc = bacc.Bacc("TRN2", target_bir_lowering=False, num_devices=1)
    args = [nc.dram_tensor(f"in_{name}", a.shape, mybir.dt.from_np(a.dtype), kind="ExternalInput").ap()
            for name, a in arrays.items()]
    out = nc.dram_tensor("out_probs", (item_id.shape[0],), mybir.dt.float32, kind="ExternalOutput").ap()
    build_rec_head(nc, *args, out)
    r = run_bass_kernel_spmd(nc, [{f"in_{name}": a for name, a in arrays.items()}], core_ids=[0])
    return r.results[0]["out_probs"]
```

```python
from contextlib import ExitStack

import concourse.bass as bass
from concourse import mybir

P = 128
NODES = 6
HEADS = 4
FIRST_ROWS = 42
LATE_FROM = 2
SLOTS = 2
LN_EPS = BN_EPS = 1e-5


def build_rec_head(nc, ids, item_mm, cates, item_emb, cate_emb, mm_w, mm_b, ln_g, ln_b, gnn_W, gnn_a,
                   se_w1, se_b1, se_w2, se_b2, bi_W, mlp_w1, mlp_b1, bn1_g, bn1_b, mlp_w2, mlp_b2,
                   bn2_g, bn2_b, mlp_w3, mlp_b3, out):
    fp32, int32 = mybir.dt.float32, mybir.dt.int32
    ALU, ACT, AX = mybir.AluOpType, mybir.ActivationFunctionType, mybir.AxisListType

    B, L = ids.shape[0], ids.shape[1] - 1
    ZERO_ROW = item_emb.shape[0] - 1
    D = item_emb.shape[1]
    CATES = cate_emb.shape[0]
    HD = D // HEADS
    TILES = B // P
    PAIRS = NODES * (NODES - 1) // 2
    KC = NODES + PAIRS
    H1, H2 = mlp_w1.shape[1], mlp_w2.shape[1]
    SE = se_w1.shape[1]
    REAL = NODES - 1
    SC = 2 * HEADS
    LAST = TILES // SLOTS - 1
    PAIR0 = [sum(NODES - 1 - a for a in range(i)) for i in range(NODES)]

    ctx = ExitStack()
    with ctx:
        def sb(name, shape, dt=fp32):
            return ctx.enter_context(nc.sbuf_tensor(name, shape, dt))

        def ps(name, width):
            return ctx.enter_context(nc.psum_tensor(name, [P, width], fp32))

        def sem(name):
            return ctx.enter_context(nc.semaphore(name))

        ident = sb("ident", [P, P])
        cate_no_i = sb("cate_no_i", [CATES, 1], int32)
        cate_no = sb("cate_no", [CATES, 1])
        cate_sb = sb("cate_sb", [CATES, D])
        mmw_sb = sb("mmw_sb", [P, D])
        mmb_bc = sb("mmb_bc", [P, D])
        lng_bc = sb("lng_bc", [P, D])
        lnb_bc = sb("lnb_bc", [P, D])
        gnn_sb = sb("gnn_sb", [P, HEADS, HD])
        a_bc = sb("a_bc", [P, HEADS, 2, HD])
        score_w = sb("score_w", [P, 2, HEADS])
        se1_raw = sb("se1_raw", [P, NODES, SE])
        se2_raw = sb("se2_raw", [P, SE, NODES])
        se1_w = sb("se1_w", [P, SE, NODES + 1])
        se2_w = sb("se2_w", [P, NODES, SE + 1])
        bi_sb = sb("bi_sb", [P, REAL, D])
        w1_sb = sb("w1_sb", [P, KC, H1])
        w2_sb = sb("w2_sb", [P, H1 // P, H2])
        bn1g_bc = sb("bn1g_bc", [P, H1])
        bias1_bc = sb("bias1_bc", [P, H1])
        bn2g_bc = sb("bn2g_bc", [P, H2])
        bias2_bc = sb("bias2_bc", [P, H2])
        w3_bc = sb("w3_bc", [P, H2])
        b3_bc = sb("b3_bc", [P, 1])

        ids_raw = sb("ids_raw", [P, SLOTS, L + 1], int32)
        ids_use = sb("ids_use", [P, SLOTS, L + 1], int32)
        is_pad = sb("is_pad", [P, SLOTS, L])
        count = sb("count", [P, SLOTS, 1])
        inv_count = sb("inv_count", [P, SLOTS, 1])
        mm_sb = sb("mm_sb", [P, SLOTS, D])
        cates_sb = sb("cates_sb", [CATES, SLOTS, 2, P], int32)
        rows = sb("rows", [P, SLOTS, L + 1, D])

        onehot = sb("onehot", [CATES, 2, P])
        mmT = sb("mmT", [P, P])
        ln_stats = sb("ln_stats", [P, 6])
        ln_mv = sb("ln_mv", [P, 2])
        ln_eps = sb("ln_eps", [P, 1])
        unused = sb("unused", [P, 1])
        ln_std = sb("ln_std", [P, 1])
        ln_rstd = sb("ln_rstd", [P, 1])
        img_pre = sb("img_pre", [P, D])
        hist_sum = sb("hist_sum", [P, D])
        mix = sb("mix", [P, SLOTS, NODES, NODES, D])
        xT = sb("xT", [P, REAL, P])
        scores = sb("scores", [P, NODES, SC])
        e = sb("e", [P, NODES, NODES, HEADS])
        att = sb("att", [P, NODES, NODES, HEADS])
        e_max = sb("e_max", [P, NODES, HEADS])
        att_sum = sb("att_sum", [P, NODES, HEADS])
        elu_e = sb("elu_e", [P, NODES, D])
        g = sb("g", [P, NODES, D])
        z = sb("z", [P, 1, NODES + 1])
        wa = sb("wa", [P, 2, HEADS, HD])
        se_p1 = sb("se_p1", [P, SE, NODES + 1])
        se_h = sb("se_h", [P, 1, SE + 1])
        se_p2 = sb("se_p2", [P, NODES, SE + 1])
        se_a = sb("se_a", [P, NODES])
        se_e = sb("se_e", [P, NODES])
        se_d = sb("se_d", [P, NODES])
        s = sb("s", [P, NODES, D])
        gT = sb("gT", [P, NODES, P])
        sT = sb("sT", [P, NODES, P])
        pairT = sb("pairT", [P, PAIRS, P])
        h1 = sb("h1", [P, H1])
        h1T = sb("h1T", [P, H1 // P, P])
        h2w = sb("h2w", [P, H2])
        logits = sb("logits", [P, TILES])
        probs = sb("probs", [P, TILES])
        outT = sb("outT", [TILES, P])

        ps_x = ps("ps_x", 512)
        ps_cate = ps("ps_cate", 512)
        ps_h1 = ps("ps_h1", H1)
        ps_hp = ps("ps_hp", 1024)
        ps_gs = ps("ps_gs", 1536)
        ps_y = ps_x[:, D:2 * D]
        ATT = NODES * NODES * HEADS
        leaky = ps_cate[:, 0:ATT].rearrange("p (n m h) -> p n m h", n=NODES, m=NODES)
        att_inv = ps_cate[:, ATT:ATT + NODES * HEADS].rearrange("p (n h) -> p n h", n=NODES)
        gate = ps_cate[:, 2 * ATT:2 * ATT + NODES]
        v = ps_gs[:, 0:NODES * D].rearrange("p (n d) -> p n d", n=NODES)
        ps_h2 = ps_gs[:, 1024:1024 + H2]
        ps_sc = ps_hp[:, REAL * D:REAL * D + REAL * SC]

        ids_loaded = [sem(f"ids_loaded{j}") for j in range(SLOTS)]
        mm_loaded = [sem(f"mm_loaded{j}") for j in range(SLOTS)]
        cates_loaded = [sem(f"cates_loaded{j}") for j in range(SLOTS)]
        id_row_landed = [sem(f"id_row_landed{j}") for j in range(SLOTS)]
        rows_a_landed = [sem(f"rows_a_landed{j}") for j in range(SLOTS)]
        rows_b_landed = [sem(f"rows_b_landed{j}") for j in range(SLOTS)]
        gathers_begun = sem("gathers_begun")
        loads_begun = sem("loads_begun")
        small_loaded = sem("small_loaded")
        w1_loaded = sem("w1_loaded")
        out_stored = sem("out_stored")
        zeros_made = sem("zeros_made")
        ident_made = sem("ident_made")
        cate_no_made = sem("cate_no_made")
        prep_step = sem("prep_step")
        weights_ready = sem("weights_ready")
        pad_known = sem("pad_known")
        pad_counted = sem("pad_counted")
        count_ready = sem("count_ready")
        ids_ready = sem("ids_ready")
        onehot_ready = sem("onehot_ready")
        mmT_ready = sem("mmT_ready")
        mmT_copied = sem("mmT_copied")
        y_ready = sem("y_ready")
        stats_ready = sem("stats_ready")
        meanvar_ready = sem("meanvar_ready")
        std_ready = sem("std_ready")
        rstd_ready = sem("rstd_ready")
        centred = sem("centred")
        img_pre_ready = sem("img_pre_ready")
        img_ready = sem("img_ready")
        cate_rows_ready = sem("cate_rows_ready")
        cate_rows_copied = sem("cate_rows_copied")
        idimgT_ready = sem("idimgT_ready")
        idimgT_copied = sem("idimgT_copied")
        rows_a_summed = sem("rows_a_summed")
        rows_summed = sem("rows_summed")
        hist_ready = sem("hist_ready")
        histT_ready = sem("histT_ready")
        histT_copied = sem("histT_copied")
        hp_ready = sem("hp_ready")
        scores_copied = sem("scores_copied")
        e_summed = sem("e_summed")
        e_leaky = sem("e_leaky")
        e_max_ready = sem("e_max_ready")
        e_shifted = sem("e_shifted")
        att_exp_ready = sem("att_exp_ready")
        att_summed = sem("att_summed")
        att_inv_ready = sem("att_inv_ready")
        att_ready = sem("att_ready")
        mixed = sem("mixed")
        v_ready = sem("v_ready")
        negpart_ready = sem("negpart_ready")
        elu_exp_ready = sem("elu_exp_ready")
        g_ready = sem("g_ready")
        z_ready = sem("z_ready")
        se_p1_ready = sem("se_p1_ready")
        se_h_ready = sem("se_h_ready")
        se_p2_ready = sem("se_p2_ready")
        se_a_ready = sem("se_a_ready")
        se_e_ready = sem("se_e_ready")
        se_d_ready = sem("se_d_ready")
        gate_ready = sem("gate_ready")
        s_ready = sem("s_ready")
        gT_ready = sem("gT_ready")
        gT_copied = sem("gT_copied")
        sT_ready = sem("sT_ready")
        sT_copied = sem("sT_copied")
        bilinear_ready = sem("bilinear_ready")
        pairs_ready = [sem(f"pairs_ready{i}") for i in range(REAL)]
        h1_pre_ready = sem("h1_pre_ready")
        h1_ready = sem("h1_ready")
        h1T_ready = sem("h1T_ready")
        h1T_copied = sem("h1T_copied")
        h2_pre_ready = sem("h2_pre_ready")
        h2_ready = sem("h2_ready")
        h2_weighted = sem("h2_weighted")
        logits_ready = sem("logits_ready")
        probs_ready = sem("probs_ready")
        probsT_ready = sem("probsT_ready")
        outT_ready = sem("outT_ready")

        def value(eng, x):
            return x if isinstance(x, int) else eng.snap(x)

        def over_tiles(eng, tile):
            for j in range(SLOTS):
                tile(0, j, j == 0, False)
            with eng.Fori(1, LAST) as i:
                for j in range(SLOTS):
                    tile(i, j, False, False)
            for j in range(SLOTS):
                tile(LAST, j, False, True)

        def preceding(i, j):
            return (i, j - 1) if j else (i - 1, SLOTS - 1)

        def following(i, j):
            return (i, j + 1) if j + 1 < SLOTS else (i + 1, 0)

        small_loads = [
            (cate_sb[:], cate_emb),
            (mmw_sb[:], mm_w),
            (mmb_bc[:], mm_b.partition_broadcast(P)),
            (lng_bc[:], ln_g.partition_broadcast(P)),
            (lnb_bc[:], ln_b.partition_broadcast(P)),
            (gnn_sb[:], gnn_W.rearrange("h i o -> i h o")),
            (a_bc[:].rearrange("p h t o -> p (h t o)"),
             gnn_a.rearrange("h t one -> (h t one)").partition_broadcast(P)),
            (se1_raw[:].rearrange("p n k -> p (n k)"), se_w1.rearrange("n k -> (n k)").partition_broadcast(P)),
            (se2_raw[:].rearrange("p k n -> p (k n)"), se_w2.rearrange("k n -> (k n)").partition_broadcast(P)),
            (z[:, 0, 0:SE], se_b1.partition_broadcast(P)),
            (se_a[:], se_b2.partition_broadcast(P)),
            (bi_sb[:], bi_W.rearrange("n d e -> d n e")),
            (w2_sb[:], mlp_w2.rearrange("(k p) n -> p k n", p=P)),
            (bn1g_bc[:], bn1_g.partition_broadcast(P)),
            (bias1_bc[:], mlp_b1.partition_broadcast(P)),
            (h1[:], bn1_b.partition_broadcast(P)),
            (bn2g_bc[:], bn2_g.partition_broadcast(P)),
            (bias2_bc[:], mlp_b2.partition_broadcast(P)),
            (h2w[:], bn2_b.partition_broadcast(P)),
            (w3_bc[:], mlp_w3.rearrange("k one -> (k one)").partition_broadcast(P)),
            (b3_bc[:], mlp_b3.partition_broadcast(P)),
        ]

        block = ctx.enter_context(nc.Block())

        @block.sync
        def _(sp):
            def load_ids(row, j):
                sp.dma_start(ids_raw[:, j, :], ids[bass.ds(row, P), :]).then_inc(ids_loaded[j], 16)

            def load_mm(row, j):
                sp.dma_start(mm_sb[:, j, :], item_mm[bass.ds(row, P), :]).then_inc(mm_loaded[j], 16)

            def load_cates(row, j):
                sp.dma_start(cates_sb[:, j, :, :],
                             cates[:, bass.ds(row, P)].partition_broadcast(CATES)).then_inc(cates_loaded[j], 16)

            for j in range(SLOTS):
                load_ids(j * P, j)
            for j in range(SLOTS):
                load_mm(j * P, j)
                load_cates(j * P, j)

            with sp.Fori(0, LAST) as i:
                for j in range(SLOTS):
                    n = value(sp, SLOTS * i + j + 1)
                    row = value(sp, (SLOTS * (i + 1) + j) * P)
                    sp.wait_ge(ids_ready, n)
                    sp.sem_inc(loads_begun, 1)
                    load_ids(row, j)
                    sp.wait_ge(mmT_ready, n)
                    sp.sem_inc(loads_begun, 1)
                    load_mm(row, j)
                    sp.wait_ge(onehot_ready, n)
                    sp.sem_inc(loads_begun, 1)
                    load_cates(row, j)
            sp.wait_ge(outT_ready, 1)
            sp.dma_start(out.rearrange("(t p) -> t p", p=P), outT[:]).then_inc(out_stored, 16)
            sp.wait_ge(out_stored, 16)

        @block.gpsimd
        def _(pool):
            nc.gpsimd.memset(ident[:], 0.0).then_inc(zeros_made, 1)
            pool.wait_ge(zeros_made, 1)
            nc.gpsimd.affine_select(out=ident[:], in_=ident[:], compare_op=ALU.not_equal, fill=1.0, base=0,
                                    pattern=[[-1, P]], channel_multiplier=1).then_inc(ident_made, 1)
            nc.gpsimd.iota(cate_no_i[:], pattern=[[0, 1]], base=0, channel_multiplier=1).then_inc(cate_no_made, 1)

            def gather(dst, j, column):
                return nc.gpsimd.indirect_dma_start(
                    out=dst, out_offset=None, in_=item_emb,
                    in_offset=bass.IndirectOffsetOnAxis(ap=ids_use[:, j, column:column + 1], axis=0))

            def tile(i, j, first, last):
                pool.wait_ge(ids_ready, value(pool, SLOTS * i + j + 1))
                pool.sem_inc(gathers_begun, 1)
                gather(mix[:, j, 3, 0, :], j, 0).then_inc(id_row_landed[j], 16)
                for k in range(FIRST_ROWS):
                    gather(rows[:, j, k, :], j, 1 + k).then_inc(rows_a_landed[j], 16)
                for k in range(FIRST_ROWS, L):
                    gather(rows[:, j, k, :], j, 1 + k).then_inc(rows_b_landed[j], 16)

            over_tiles(pool, tile)

        @block.scalar
        def _(act):
            for dst, src in small_loads:
                act.dma_start(dst, src).then_inc(small_loaded, 16)
            act.dma_start(w1_sb[:], mlp_w1.rearrange("(k p) n -> p k n", p=P)).then_inc(w1_loaded, 16)
            act.wait_ge(weights_ready, 1)

            def bring_table(function):
                nc.scalar.activation(unused[:], ln_eps[:], function)

            def early(i, j):
                n = value(act, SLOTS * i + j + 1)
                act.wait_ge(mmT_ready, n)
                nc.scalar.copy(mmT[:], ps_x[:, 0:P]).then_inc(mmT_copied, 1)
                act.wait_ge(cate_rows_ready, n)
                nc.scalar.copy(mix[:, j, 1:3, 0, :], ps_cate[:, 0:2 * D].rearrange("p (n d) -> p n d", n=2))
                nc.scalar.copy(xT[:, 0:2, :], ps_cate[:, 2 * D:4 * D].rearrange("p (n d) -> p n d", n=2)
                               ).then_inc(cate_rows_copied, 1)
                act.wait_ge(meanvar_ready, n)
                nc.scalar.activation(ln_std[:], ln_mv[:, 1:2], ACT.Sqrt, bias=ln_eps[:, 0:1]).then_inc(std_ready, 1)
                act.wait_ge(img_pre_ready, n)
                nc.scalar.activation(mix[:, j, 4, 0, :], img_pre[:], ACT.Gelu).then_inc(img_ready, 1)
                act.wait_ge(idimgT_ready, n)
                nc.scalar.copy(xT[:, 2:4, :], ps_x[:, 2 * P:4 * P].rearrange("p (n s) -> p n s", n=2)
                               ).then_inc(idimgT_copied, 1)
                bring_table(ACT.Exp)

            def hidden_layers(i, j):
                n = value(act, SLOTS * i + j + 1)
                act.wait_ge(h1_pre_ready, n)
                nc.scalar.activation(h1[:], ps_h1[:], ACT.Gelu).then_inc(h1_ready, 1)
                act.wait_ge(h1T_ready, n)
                nc.scalar.copy(h1T[:].rearrange("p k s -> p (k s)"), ps_h1[:]).then_inc(h1T_copied, 1)
                act.wait_ge(h2_pre_ready, n)
                nc.scalar.activation(ps_h2, ps_h2, ACT.Gelu).then_inc(h2_ready, 1)

            def tile(i, j, first, last):
                n = value(act, SLOTS * i + j + 1)
                act.wait_ge(histT_ready, n)
                nc.scalar.copy(xT[:, 4, :], ps_x[:, 0:P]).then_inc(histT_copied, 1)
                act.wait_ge(e_shifted, n)
                nc.scalar.activation(att[:], leaky, ACT.Exp).then_inc(att_exp_ready, 1)
                if not first:
                    hidden_layers(*preceding(i, j))
                    bring_table(ACT.Exp)
                act.wait_ge(v_ready, n)
                nc.scalar.activation(elu_e[:], v, ACT.Relu, scale=-1.0).then_inc(negpart_ready, 1)
                act.wait_ge(negpart_ready, n)
                nc.scalar.activation(elu_e[:], elu_e[:], ACT.Exp, scale=-1.0).then_inc(elu_exp_ready, 1)
                act.wait_ge(gT_ready, n)
                nc.scalar.copy(gT[:].rearrange("p n s -> p (n s)"), ps_gs[:, 0:NODES * P]).then_inc(gT_copied, 1)
                act.wait_ge(se_a_ready, n)
                nc.scalar.activation(se_e[:], se_a[:], ACT.Exp, scale=-1.0).then_inc(se_e_ready, 1)
                if not last or j + 1 < SLOTS:
                    early(*following(i, j))

            early(0, 0)
            over_tiles(act, tile)
            hidden_layers(LAST, SLOTS - 1)
            bring_table(ACT.Sigmoid)
            act.wait_ge(logits_ready, TILES)
            nc.scalar.activation(probs[:], logits[:], ACT.Sigmoid, bias=b3_bc[:, 0:1]).then_inc(probs_ready, 1)
            act.wait_ge(probsT_ready, 1)
            nc.scalar.copy(outT[:], ps_x[0:TILES, 0:P]).then_inc(outT_ready, 1)

        @block.vector
        def _(dve):
            def make_ids(n, count_loaded, j):
                dve.wait_ge(ids_loaded[j], count_loaded)
                nc.vector.tensor_scalar(is_pad[:, j, :], ids_raw[:, j, 1:L + 1], 0.0, None, ALU.is_equal
                                        ).then_inc(pad_known, 1)
                nc.vector.tensor_copy(ids_use[:, j, 0:1], ids_raw[:, j, 0:1])
                dve.wait_ge(pad_known, n)
                nc.vector.tensor_reduce(count[:, j, :], is_pad[:, j, :], AX.X, ALU.add, negate=True
                                        ).then_inc(pad_counted, 1)
                nc.vector.scalar_tensor_tensor(ids_use[:, j, 1:L + 1], is_pad[:, j, :], float(ZERO_ROW),
                                               ids_raw[:, j, 1:L + 1], ALU.mult, ALU.add)
                dve.wait_ge(pad_counted, n)
                nc.vector.tensor_scalar(count[:, j, :], count[:, j, :], float(L), 1.0, ALU.add, ALU.max
                                        ).then_inc(count_ready, 1)
                dve.wait_ge(count_ready, n)
                nc.vector.reciprocal(inv_count[:, j, :], count[:, j, :]).then_inc(ids_ready, 1)

            for j in range(SLOTS):
                make_ids(j + 1, 16, j)

            nc.vector.memset(mix[:, :, 0, 0, :], 0.0)
            nc.vector.memset(scores[:, 0, :], 0.0)
            nc.vector.memset(se_h[:], 1.0)
            nc.vector.memset(ln_eps[:], LN_EPS)
            dve.wait_ge(cate_no_made, 1)
            nc.vector.tensor_copy(cate_no[:], cate_no_i[:])
            dve.wait_ge(small_loaded, 16 * len(small_loads))
            scale = float(1.0 / (1.0 + BN_EPS) ** 0.5)
            nc.vector.tensor_scalar(bn1g_bc[:], bn1g_bc[:], scale, None, ALU.mult)
            nc.vector.tensor_scalar(bn2g_bc[:], bn2g_bc[:], scale, None, ALU.mult)
            nc.vector.tensor_scalar(se1_w[:, :, 0:NODES], se1_raw[:].rearrange("p n k -> p k n"), 1.0 / D, None,
                                    ALU.mult)
            nc.vector.tensor_copy(se1_w[:, :, NODES], z[:, 0, 0:SE])
            nc.vector.tensor_copy(se2_w[:, :, 0:SE], se2_raw[:].rearrange("p k n -> p n k"))
            nc.vector.tensor_copy(se2_w[:, :, SE], se_a[:])
            for t in range(2):
                nc.vector.tensor_tensor(wa[:, t, :, :], gnn_sb[:], a_bc[:, :, t, :], ALU.mult).then_inc(prep_step, 1)
            dve.wait_ge(prep_step, 2)
            nc.vector.memset(z[:], 1.0)
            for t in range(2):
                nc.vector.tensor_reduce(score_w[:, t, :], wa[:, t, :, :], AX.X, ALU.add)
            nc.vector.tensor_tensor(bias1_bc[:], bias1_bc[:], bn1g_bc[:], ALU.mult).then_inc(prep_step, 1)
            nc.vector.tensor_tensor(bias2_bc[:], bias2_bc[:], bn2g_bc[:], ALU.mult).then_inc(prep_step, 1)
            dve.wait_ge(prep_step, 4)
            nc.vector.tensor_tensor(bias1_bc[:], bias1_bc[:], h1[:], ALU.add)
            nc.vector.tensor_tensor(bias2_bc[:], bias2_bc[:], h2w[:], ALU.add)
            nc.vector.tensor_tensor(w2_sb[:], w2_sb[:], bn2g_bc[:].unsqueeze(1).to_broadcast([P, H1 // P, H2]),
                                    ALU.mult)
            dve.wait_ge(w1_loaded, 16)
            nc.vector.tensor_tensor(w1_sb[:], w1_sb[:], bn1g_bc[:].unsqueeze(1).to_broadcast([P, KC, H1]),
                                    ALU.mult).then_inc(weights_ready, 1)

            def early(i, j):
                n = value(dve, SLOTS * i + j + 1)
                loaded = value(dve, 16 * (i + 1))
                dve.wait_ge(y_ready, n)
                nc.vector.bn_stats(ln_stats[:], ps_y).then_inc(stats_ready, 1)
                dve.wait_ge(cates_loaded[j], loaded)
                dve.wait_ge(stats_ready, n)
                nc.vector.tensor_scalar(onehot[:], cates_sb[:, j, :, :], cate_no[:, 0:1], None, ALU.is_equal
                                        ).then_inc(onehot_ready, 1)
                nc.vector.bn_aggr(ln_mv[:], ln_stats[:]).then_inc(meanvar_ready, 1)
                dve.wait_ge(meanvar_ready, n)
                nc.vector.scalar_tensor_tensor(ps_y, ps_y, ln_mv[:, 0:1], lng_bc[:], ALU.subtract, ALU.mult
                                               ).then_inc(centred, 1)
                dve.wait_ge(std_ready, n)
                nc.vector.reciprocal(ln_rstd[:], ln_std[:]).then_inc(rstd_ready, 1)
                dve.wait_ge(centred, n)
                dve.wait_ge(rstd_ready, n)
                nc.vector.scalar_tensor_tensor(img_pre[:], ps_y, ln_rstd[:, 0:1], lnb_bc[:], ALU.mult, ALU.add
                                               ).then_inc(img_pre_ready, 1)

            def sum_first_rows(i, j):
                dve.wait_ge(rows_a_landed[j], value(dve, 16 * FIRST_ROWS * (i + 1)))
                nc.vector.tensor_reduce(rows[:, j, L, :], rows[:, j, 0:FIRST_ROWS, :].rearrange("p l d -> p d l"),
                                        AX.X, ALU.add).then_inc(rows_a_summed, 1)

            def score_last_layer(i, j):
                n = value(dve, SLOTS * i + j + 1)
                dve.wait_ge(h2_ready, n)
                nc.vector.tensor_tensor(h2w[:], ps_h2, w3_bc[:], ALU.mult).then_inc(h2_weighted, 1)
                dve.wait_ge(h2_weighted, n)
                t = value(dve, SLOTS * i + j)
                nc.vector.tensor_reduce(logits[:, bass.ds(t, 1)], h2w[:], AX.X, ALU.add).then_inc(logits_ready, 1)

            def tile(i, j, first, last):
                n = value(dve, SLOTS * i + j + 1)
                dve.wait_ge(rows_b_landed[j], value(dve, 16 * (L - FIRST_ROWS) * (i + 1)))
                dve.wait_ge(rows_a_summed, n)
                nc.vector.tensor_reduce(hist_sum[:], rows[:, j, FIRST_ROWS:L + 1, :].rearrange("p l d -> p d l"),
                                        AX.X, ALU.add).then_inc(rows_summed, 1)
                dve.wait_ge(rows_summed, n)
                nc.vector.tensor_scalar(mix[:, j, 5, 0, :], hist_sum[:], inv_count[:, j, 0:1], None, ALU.mult
                                        ).then_inc(hist_ready, 1)

                dve.wait_ge(hp_ready, n)
                nc.vector.tensor_copy(scores[:, 1:NODES, :], ps_sc.rearrange("p (n c) -> p n c", c=SC)
                                      ).then_inc(scores_copied, 1)
                dve.wait_ge(scores_copied, n)
                nc.vector.tensor_tensor(
                    e[:], scores[:, :, 0:HEADS].unsqueeze(2).to_broadcast([P, NODES, NODES, HEADS]),
                    scores[:, :, HEADS:SC].unsqueeze(1).to_broadcast([P, NODES, NODES, HEADS]), ALU.add
                ).then_inc(e_summed, 1)
                dve.wait_ge(e_summed, n)
                nc.vector.scalar_tensor_tensor(leaky, e[:], 0.2, e[:], ALU.mult, ALU.max).then_inc(e_leaky, 1)
                dve.wait_ge(e_leaky, n)
                nc.vector.tensor_reduce(e_max[:], leaky.rearrange("p n m h -> p n h m"), AX.X, ALU.max
                                        ).then_inc(e_max_ready, 1)
                dve.wait_ge(e_max_ready, n)
                nc.vector.tensor_tensor(leaky, leaky, e_max[:].unsqueeze(2).to_broadcast([P, NODES, NODES, HEADS]),
                                        ALU.subtract).then_inc(e_shifted, 1)
                dve.wait_ge(att_exp_ready, n)
                nc.vector.tensor_reduce(att_sum[:], att[:].rearrange("p n m h -> p n h m"), AX.X, ALU.add
                                        ).then_inc(att_summed, 1)
                dve.wait_ge(att_summed, n)
                nc.vector.reciprocal(att_inv, att_sum[:]).then_inc(att_inv_ready, 1)
                dve.wait_ge(att_inv_ready, n)
                nc.vector.tensor_tensor(att[:], att[:], att_inv.unsqueeze(2).to_broadcast([P, NODES, NODES, HEADS]),
                                        ALU.mult).then_inc(att_ready, 1)

                dve.wait_ge(att_ready, n)
                nc.vector.tensor_tensor(
                    mix[:, j, :, 1:NODES, :].rearrange("p n m (h o) -> p n (m h) o", h=HEADS),
                    att[:, :, 1:NODES, :].rearrange("p n m h -> p n (m h)").unsqueeze(3).to_broadcast(
                        [P, NODES, REAL * HEADS, HD]),
                    ps_hp[:, 0:REAL * D].rearrange("p (a o) -> p a o", o=HD).unsqueeze(1).to_broadcast(
                        [P, NODES, REAL * HEADS, HD]), ALU.mult).then_inc(mixed, 1)
                dve.wait_ge(mixed, n)
                nc.vector.tensor_reduce(v, mix[:, j, :, :, :].rearrange("p n m d -> p n d m"), AX.X, ALU.add
                                        ).then_inc(v_ready, 1)

                if not first:
                    score_last_layer(*preceding(i, j))
                if not last:
                    dve.wait_ge(v_ready, n)
                    make_ids(value(dve, SLOTS * (i + 1) + j + 1), value(dve, 16 * (i + 2)), j)

                dve.wait_ge(elu_exp_ready, n)
                nc.vector.scalar_tensor_tensor(g[:], elu_e[:], -1.0, v, ALU.add, ALU.max).then_inc(g_ready, 1)

                dve.wait_ge(g_ready, n)
                nc.vector.tensor_reduce(z[:, 0, 0:NODES], g[:], AX.X, ALU.add).then_inc(z_ready, 1)
                dve.wait_ge(z_ready, n)
                nc.vector.tensor_tensor(se_p1[:], z[:].to_broadcast([P, SE, NODES + 1]), se1_w[:], ALU.mult
                                        ).then_inc(se_p1_ready, 1)
                dve.wait_ge(se_p1_ready, n)
                nc.vector.tensor_reduce(se_h[:, 0, 0:SE], se_p1[:], AX.X, ALU.add).then_inc(se_h_ready, 1)
                dve.wait_ge(se_h_ready, n)
                nc.vector.scalar_tensor_tensor(se_p2[:], se_h[:].to_broadcast([P, NODES, SE + 1]), 0.0, se2_w[:],
                                               ALU.max, ALU.mult).then_inc(se_p2_ready, 1)
                dve.wait_ge(se_p2_ready, n)
                nc.vector.tensor_reduce(se_a[:], se_p2[:], AX.X, ALU.add).then_inc(se_a_ready, 1)
                dve.wait_ge(se_e_ready, n)
                nc.vector.tensor_scalar(se_d[:], se_e[:], 1.0, None, ALU.add).then_inc(se_d_ready, 1)
                dve.wait_ge(se_d_ready, n)
                nc.vector.reciprocal(gate, se_d[:]).then_inc(gate_ready, 1)
                dve.wait_ge(gate_ready, n)
                nc.vector.tensor_tensor(s[:], g[:], gate.unsqueeze(2).to_broadcast([P, NODES, D]), ALU.mult
                                        ).then_inc(s_ready, 1)
                dve.wait_ge(sT_ready, n)
                nc.vector.tensor_copy(sT[:].rearrange("p n s -> p (n s)"), ps_gs[:, NODES * P:2 * NODES * P]
                                      ).then_inc(sT_copied, 1)

                dve.wait_ge(bilinear_ready, n)
                dve.wait_ge(sT_copied, n)
                for a in range(REAL):
                    others = NODES - 1 - a
                    nc.vector.tensor_tensor(
                        pairT[:, PAIR0[a]:PAIR0[a] + others, :],
                        ps_hp[:, a * P:(a + 1) * P].unsqueeze(1).to_broadcast([P, others, P]),
                        sT[:, a + 1:NODES, :], ALU.mult).then_inc(pairs_ready[a], 1)

                if not last or j + 1 < SLOTS:
                    early(*following(i, j))
                    sum_first_rows(*following(i, j))

            early(0, 0)
            sum_first_rows(0, 0)
            over_tiles(dve, tile)
            score_last_layer(LAST, SLOTS - 1)

        @block.tensor
        def _(pe):
            pe.wait_ge(ident_made, 1)
            pe.wait_ge(weights_ready, 1)

            def project(m):
                nc.tensor.matmul(ps_hp[:, m * D:(m + 1) * D], xT[:, m, :],
                                 gnn_sb[:].rearrange("p h o -> p (h o)"), start=True, stop=True)
                return nc.tensor.matmul(ps_sc[:, m * SC:(m + 1) * SC], xT[:, m, :],
                                        score_w[:].rearrange("p t h -> p (t h)"), start=True, stop=True)

            def transpose_image_rows(i, j):
                pe.wait_ge(mm_loaded[j], value(pe, 16 * (i + 1)))
                nc.tensor.transpose(ps_x[:, 0:P], mm_sb[:, j, :], ident[:]).then_inc(mmT_ready, 1)

            def project_image(i, j):
                pe.wait_ge(mmT_copied, value(pe, SLOTS * i + j + 1))
                nc.tensor.matmul(ps_y, ident[:], mmb_bc[:], start=True, stop=False)
                nc.tensor.matmul(ps_y, mmT[:], mmw_sb[:], start=False, stop=True).then_inc(y_ready, 1)

            def look_up_cates(i, j):
                pe.wait_ge(onehot_ready, value(pe, SLOTS * i + j + 1))
                for k in range(2):
                    nc.tensor.matmul(ps_cate[:, k * D:(k + 1) * D], onehot[:, k, :], cate_sb[:], start=True, stop=True)
                nc.tensor.matmul(ps_cate[:, 2 * D:4 * D], cate_sb[:], onehot[:].rearrange("c k s -> c (k s)"),
                                 start=True, stop=True).then_inc(cate_rows_ready, 1)

            def transpose_id_and_image(i, j):
                pe.wait_ge(id_row_landed[j], value(pe, 16 * (i + 1)))
                pe.wait_ge(img_ready, value(pe, SLOTS * i + j + 1))
                nc.tensor.transpose(ps_x[:, 2 * P:3 * P], mix[:, j, 3, 0, :], ident[:])
                nc.tensor.transpose(ps_x[:, 3 * P:4 * P], mix[:, j, 4, 0, :], ident[:]).then_inc(idimgT_ready, 1)

            def project_first_nodes(i, j):
                n = value(pe, SLOTS * i + j + 1)
                pe.wait_ge(cate_rows_copied, n)
                pe.wait_ge(idimgT_copied, n)
                for m in range(REAL - 1):
                    project(m)

            def layer1(lhsT, k, stop=False):
                return nc.tensor.matmul(ps_h1[:], lhsT, w1_sb[:, k, :], start=False, stop=stop)

            def late_pairs(i, j):
                n = value(pe, SLOTS * i + j + 1)
                for a in range(LATE_FROM, REAL):
                    pe.wait_ge(pairs_ready[a], n)
                    for k in range(PAIR0[a], PAIR0[a + 1]):
                        step = layer1(pairT[:, k, :], NODES + k, stop=k == PAIRS - 1)
                step.then_inc(h1_pre_ready, 1)

            def second_layer(i, j):
                n = value(pe, SLOTS * i + j + 1)
                pe.wait_ge(h1_ready, n)
                nc.tensor.matmul(ps_h2, ident[:], bias2_bc[:], start=True, stop=False)
                for k in range(H1 // P):
                    step = nc.tensor.transpose(ps_h1[:, k * P:(k + 1) * P], h1[:, k * P:(k + 1) * P], ident[:])
                step.then_inc(h1T_ready, 1)
                pe.wait_ge(h1T_copied, n)
                for k in range(H1 // P):
                    step = nc.tensor.matmul(ps_h2, h1T[:, k, :], w2_sb[:, k, :], start=False, stop=k == H1 // P - 1)
                step.then_inc(h2_pre_ready, 1)

            def tile(i, j, first, last):
                n = value(pe, SLOTS * i + j + 1)
                pe.wait_ge(hist_ready, n)
                nc.tensor.transpose(ps_x[:, 0:P], mix[:, j, 5, 0, :], ident[:]).then_inc(histT_ready, 1)
                pe.wait_ge(histT_copied, n)
                project(REAL - 1).then_inc(hp_ready, 1)
                if not first:
                    late_pairs(*preceding(i, j))
                    second_layer(*preceding(i, j))

                nc.tensor.matmul(ps_h1[:], ident[:], bias1_bc[:], start=True, stop=False)
                pe.wait_ge(g_ready, n)
                for k in range(NODES):
                    step = nc.tensor.transpose(ps_gs[:, k * P:(k + 1) * P], g[:, k, :], ident[:])
                step.then_inc(gT_ready, 1)
                pe.wait_ge(gT_copied, n)
                for k in range(NODES // 2):
                    layer1(gT[:, k, :], k)
                pe.wait_ge(s_ready, n)
                for k in range(NODES):
                    step = nc.tensor.transpose(ps_gs[:, (NODES + k) * P:(NODES + k + 1) * P], s[:, k, :], ident[:])
                step.then_inc(sT_ready, 1)
                for k in range(NODES // 2, NODES - 1):
                    layer1(gT[:, k, :], k)
                pe.wait_ge(sT_copied, n)
                for a in range(REAL):
                    step = nc.tensor.matmul(ps_hp[:, a * P:(a + 1) * P], bi_sb[:, a, :], sT[:, a, :],
                                            start=True, stop=True)
                step.then_inc(bilinear_ready, 1)
                layer1(gT[:, NODES - 1, :], NODES - 1)

                def pairs(a, start, stop):
                    for k in range(PAIR0[a] + start, PAIR0[a] + stop):
                        layer1(pairT[:, k, :], NODES + k)

                ahead = not last or j + 1 < SLOTS
                pe.wait_ge(pairs_ready[0], n)
                pairs(0, 0, 2)
                if ahead:
                    transpose_image_rows(*following(i, j))
                pairs(0, 2, 4)
                if ahead:
                    project_image(*following(i, j))
                pairs(0, 4, 5)
                pe.wait_ge(pairs_ready[1], n)
                pairs(1, 0, 1)
                if ahead:
                    look_up_cates(*following(i, j))
                pairs(1, 1, 4)
                if ahead:
                    transpose_id_and_image(*following(i, j))
                    project_first_nodes(*following(i, j))

            transpose_image_rows(0, 0)
            project_image(0, 0)
            look_up_cates(0, 0)
            transpose_id_and_image(0, 0)
            project_first_nodes(0, 0)
            over_tiles(pe, tile)
            late_pairs(LAST, SLOTS - 1)
            second_layer(LAST, SLOTS - 1)
            pe.wait_ge(probs_ready, 1)
            nc.tensor.transpose(ps_x[0:TILES, 0:P], probs[:], ident[:]).then_inc(probsT_ready, 1)


_PLAIN = ["item_emb", "cate_emb", "mm_w", "mm_b", "ln_g", "ln_b", "gnn_W", "gnn_a", "se_w1", "se_b1", "se_w2",
          "se_b2", "bi_W", "mlp_w1", "mlp_b1", "bn1_g", "bn1_b", "mlp_w2", "mlp_b2", "bn2_g", "bn2_b", "mlp_w3",
          "mlp_b3"]


def kernel(**inputs):
    import numpy as np
    import concourse.bacc as bacc
    from concourse.bass_utils import run_bass_kernel_spmd

    item_id = np.asarray(inputs["r_item_id"])
    arrays = {
        "ids": np.concatenate([item_id[:, None], np.asarray(inputs["r_item_seq"])], axis=1),
        "item_mm": np.ascontiguousarray(inputs["r_item_mm"]),
        "cates": np.stack([np.asarray(inputs["r_likes"]), np.asarray(inputs["r_views"])]),
    }
    for name in _PLAIN:
        arrays[name] = np.ascontiguousarray(inputs[f"L0_rec_{name}"])
    table = arrays["item_emb"]
    arrays["item_emb"] = np.concatenate([table, np.zeros((1, table.shape[1]), table.dtype)])

    nc = bacc.Bacc("TRN2", target_bir_lowering=False, num_devices=1)
    args = [nc.dram_tensor(f"in_{name}", a.shape, mybir.dt.from_np(a.dtype), kind="ExternalInput").ap()
            for name, a in arrays.items()]
    out = nc.dram_tensor("out_probs", (item_id.shape[0],), mybir.dt.float32, kind="ExternalOutput").ap()
    build_rec_head(nc, *args, out)
    r = run_bass_kernel_spmd(nc, [{f"in_{name}": a for name, a in arrays.items()}], core_ids=[0])
    return r.results[0]["out_probs"]
```
